# Optimizing a Trainium2 kernel written in Bass

```python
import numpy as np
import jax
import jax.numpy as jnp

def _softmax(x, axis=-1):
    return jax.nn.softmax(x, axis=axis)

def _gelu(x):
    return jax.nn.gelu(x, approximate=True)

def _silu(x):
    return jax.nn.silu(x)

def _sigmoid(x):
    return jax.nn.sigmoid(x)

def _layernorm(x, axis=-1, eps=1e-05):
    m = jnp.mean(x, axis=axis, keepdims=True)
    v = jnp.var(x, axis=axis, keepdims=True)
    return (x - m) / jnp.sqrt(v + eps)

def _scatter_add(tgt, idx, src, axis=0):
    return tgt.at[idx].add(src)

def _segment_sum(src, seg, n):
    return jax.ops.segment_sum(src, seg, n)
kernel_name = 'mk_recurrent_d1_jaxref_r4_1a1044'

def setup_inputs(seed: int=0):
    np.random.seed(seed)
    _w = jnp.asarray

    def _L0_attn_setup():
        import jax, jax.numpy as jnp
        import numpy as np
        BASE_THETA = 0.5
        K_DOP = 0.2
        K_NOR = 0.15
        K_SERO = 0.1
        DIM = 256
        key = jax.random.key(seed)
        ks = jax.random.split(key, 9)
        scale = 1.0 / np.sqrt(DIM)
        x = jax.random.normal(ks[0], (2, 512, DIM), dtype=jnp.float32)
        Wq = jax.random.normal(ks[1], (DIM, DIM), dtype=jnp.float32) * scale
        bq = jnp.zeros((DIM,), dtype=jnp.float32)
        Wk = jax.random.normal(ks[2], (DIM, DIM), dtype=jnp.float32) * scale
        bk = jnp.zeros((DIM,), dtype=jnp.float32)
        Wv = jax.random.normal(ks[3], (DIM, DIM), dtype=jnp.float32) * scale
        bv = jnp.zeros((DIM,), dtype=jnp.float32)
        Wo = jax.random.normal(ks[4], (DIM, DIM), dtype=jnp.float32) * scale
        bo = jnp.zeros((DIM,), dtype=jnp.float32)
        return {'x': x, 'Wq': Wq, 'bq': bq, 'Wk': Wk, 'bk': bk, 'Wv': Wv, 'bv': bv, 'Wo': Wo, 'bo': bo}
    _L0_attn_in = _L0_attn_setup()

    def _L0_ffn_setup():
        import jax, jax.numpy as jnp
        import numpy as np
        B, S, D, E, H = (4, 512, 256, 8, 1024)
        key = jax.random.key(seed)
        ks = jax.random.split(key, 7)
        scale_d = 1.0 / np.sqrt(D)
        scale_h = 1.0 / np.sqrt(H)
        return {'x': jax.random.normal(ks[0], (B, S, D), dtype=jnp.float32), 'Wr': jax.random.uniform(ks[1], (D, E), jnp.float32, -scale_d, scale_d), 'br': jnp.zeros((E,), jnp.float32), 'W1': jax.random.uniform(ks[2], (E, D, H), jnp.float32, -scale_d, scale_d), 'b1': jax.random.uniform(ks[3], (E, H), jnp.float32, -scale_d, scale_d), 'W2': jax.random.uniform(ks[4], (E, H, D), jnp.float32, -scale_h, scale_h), 'b2': jax.random.uniform(ks[5], (E, D), jnp.float32, -scale_h, scale_h)}
    _L0_ffn_in = _L0_ffn_setup()
    _d = {'L0_attn_x': _L0_attn_in['x'], 'L0_attn_Wq': _L0_attn_in['Wq'], 'L0_attn_bq': _L0_attn_in['bq'], 'L0_attn_Wk': _L0_attn_in['Wk'], 'L0_attn_bk': _L0_attn_in['bk'], 'L0_attn_Wv': _L0_attn_in['Wv'], 'L0_attn_bv': _L0_attn_in['bv'], 'L0_attn_Wo': _L0_attn_in['Wo'], 'L0_attn_bo': _L0_attn_in['bo'], 'L0_ffn_Wr': _L0_ffn_in['Wr'], 'L0_ffn_br': _L0_ffn_in['br'], 'L0_ffn_W1': _L0_ffn_in['W1'], 'L0_ffn_b1': _L0_ffn_in['b1'], 'L0_ffn_W2': _L0_ffn_in['W2'], 'L0_ffn_b2': _L0_ffn_in['b2']}
    _x0 = _d['L0_attn_x']
    _d['L0_attn_x'] = jax.random.normal(jax.random.fold_in(jax.random.key(seed), 1), (4, 1024, 256), dtype=_x0.dtype)
    del _x0
    return _d

def reference(L0_attn_x, L0_attn_Wq, L0_attn_bq, L0_attn_Wk, L0_attn_bk, L0_attn_Wv, L0_attn_bv, L0_attn_Wo, L0_attn_bo, L0_ffn_Wr, L0_ffn_br, L0_ffn_W1, L0_ffn_b1, L0_ffn_W2, L0_ffn_b2):

    def _L0_attn_ref(x, Wq, bq, Wk, bk, Wv, bv, Wo, bo):
        import jax, jax.numpy as jnp
        import numpy as np
        BASE_THETA = 0.5
        K_DOP = 0.2
        K_NOR = 0.15
        K_SERO = 0.1
        DIM = 256
        q = jnp.einsum('bsd,ed->bse', x, Wq) + bq
        k = jnp.einsum('bsd,ed->bse', x, Wk) + bk
        v = jnp.einsum('bsd,ed->bse', x, Wv) + bv
        qk = jnp.einsum('bsd,btd->bst', q, k)
        theta = BASE_THETA + K_DOP * jax.nn.sigmoid(qk) + K_NOR * jnp.tanh(qk) + K_SERO * jax.nn.relu(qk)
        attn = jax.nn.softmax(theta, axis=-1)
        out = jnp.einsum('bst,btd->bsd', attn, v)
        return jnp.einsum('bsd,ed->bse', out, Wo) + bo

    def _L0_ffn_ref(x, Wr, br, W1, b1, W2, b2):
        import jax, jax.numpy as jnp
        import numpy as np
        B, S, D, E, H = (4, 512, 256, 8, 1024)
        route_logits = jnp.einsum('bsd,de->bse', x, Wr) + br
        routing_weights = jax.nn.softmax(route_logits, axis=-1)
        selected_expert = jnp.argmax(routing_weights, axis=-1)
        num_experts = W1.shape[0]
        out = jnp.zeros_like(x)
        for e in range(num_experts):
            h = jax.nn.gelu(jnp.einsum('bsd,dh->bsh', x, W1[e]) + b1[e], approximate=False)
            y = jnp.einsum('bsh,hd->bsd', h, W2[e]) + b2[e]
            out = jnp.where((selected_expert == e)[..., None], y, out)
        return out
    x = L0_attn_x
    xn = _layernorm(x, axis=-1)
    s = _L0_attn_ref(xn, L0_attn_Wq, L0_attn_bq, L0_attn_Wk, L0_attn_bk, L0_attn_Wv, L0_attn_bv, L0_attn_Wo, L0_attn_bo)
    g = _silu(_L0_ffn_ref(xn, L0_ffn_Wr, L0_ffn_br, L0_ffn_W1, L0_ffn_b1, L0_ffn_W2, L0_ffn_b2))
    x = x + s * g
    return x

_drawn_inputs = setup_inputs


def setup_inputs(seed=0):
    import zlib

    import numpy as np

    out = dict(_drawn_inputs(seed))
    spreads = {'L0_attn_bq': (0.0, 0.8),
     'L0_attn_bk': (0.0, 0.8),
     'L0_attn_bv': (0.0, 0.8),
     'L0_attn_bo': (0.0, 0.8),
     'L0_ffn_br': (0.0, 0.612)}
    factors = {'L0_attn_Wq': 4.104,
     'L0_attn_Wk': 3.927,
     'L0_attn_Wv': 3.808,
     'L0_attn_Wo': 3.193,
     'L0_ffn_Wr': 3.069,
     'L0_ffn_W1': 3.018,
     'L0_ffn_b1': 8.0,
     'L0_ffn_W2': 2.841,
     'L0_ffn_b2': 8.0}
    for name, (base, spread) in spreads.items():
        noise = np.random.default_rng([zlib.crc32(name.encode()), seed]).standard_normal(out[name].shape)
        drawn = base * np.exp(spread * noise) if base else spread * noise
        out[name] = jnp.asarray(drawn.astype(out[name].dtype))
    for name, factor in factors.items():
        out[name] = (out[name] * factor).astype(out[name].dtype)
    return out
```

```python
from contextlib import ExitStack

import concourse.bass as bass
from concourse import mybir

P = 128
F32 = mybir.dt.float32
F32R = mybir.dt.float32r
I32 = mybir.dt.int32
ALU = mybir.AluOpType
ACT = mybir.ActivationFunctionType
X = mybir.AxisListType.X

LN_EPS = 1e-5
BASE_THETA, K_SIGMOID, K_TANH, K_RELU = 0.5, 0.2, 0.15, 0.1


def block_attention_moe(nc, x, Wq, bq, Wk, bk, Wv, bv, Wo, bo, Wr, br, W1, b1, W2, b2, out):
    B, S, D = x.shape
    E, _, H = W1.shape
    DC = D // P
    HC = H // P
    TPB = S // P
    NT = B * TPB
    MAX_TILES = NT + E - 1
    HALF = S // 2
    SM = E + 2
    VW = D + 2
    assert (P, DC, HALF) == (128, 2, 512) and TPB == 8

    x_rows = x.rearrange("b s d -> (b s) d")
    out_rows = out.rearrange("b s d -> (b s) d")
    sorted_x = nc.dram_tensor("sorted_x", ((MAX_TILES + 1) * P, D), F32, kind="Internal").ap()
    sorted_g = nc.dram_tensor("sorted_g", (MAX_TILES * P, D), F32, kind="Internal").ap()

    with ExitStack() as ctx:
        def sb(name, shape, dt=F32):
            return ctx.enter_context(nc.sbuf_tensor(name, shape, dt))

        def sem(name):
            return ctx.enter_context(nc.semaphore(name))

        ps = ctx.enter_context(nc.psum_tensor("ps", [P, 8, 512], F32))

        ident = sb("ident", [P, P])
        before = sb("before", [P, P])
        ones = sb("ones", [P, P])
        zeros = sb("zeros", [P, D])
        warm = sb("warm", [P, 3])
        bias_rows = sb("bias_rows", [E * HC + 3 * DC, P])
        bias_cols = sb("bias_cols", [P, E * HC + 3 * DC])
        BQ, BK, BV = E * HC, E * HC + DC, E * HC + 2 * DC
        bo_row = sb("bo_row", [1, D])
        br_all = sb("br_all", [P, E])
        b2_all = sb("b2_all", [P, E * D])
        kappa = sb("kappa", [P, 1])
        r_col = sb("r_col", [P, DC])
        attn_const = sb("attn_const", [P, D])
        M_hi, M_lo = sb("M_hi", [P, DC, D], F32R), sb("M_lo", [P, DC, D], F32R)
        G_hi, G_lo = sb("G_hi", [P, DC, D], F32R), sb("G_lo", [P, DC, D], F32R)
        R_hi, R_lo = sb("R_hi", [P, DC, SM], F32R), sb("R_lo", [P, DC, SM], F32R)
        small_w = sb("small_w", [P, DC, SM])
        xn_all = sb("xn_all", [P, NT, D])
        xn_cur = sb("xn_cur", [P, TPB, D])
        xnT_hi, xnT_lo = sb("xnT_hi", [P, DC, S], F32R), sb("xnT_lo", [P, DC, S], F32R)
        stats = sb("stats", [P, TPB, 6])
        mean_var = sb("mean_var", [P, TPB, 2])
        std = sb("std", [P, TPB])
        rstd = sb("rstd", [P, TPB])
        logits = sb("logits", [P, E, NT])
        c_all = sb("c_all", [P, NT])
        slot_i = sb("slot_i", [P, NT], I32)
        first_tile = sb("first_tile", [P, E + 1], I32)
        qkvo_in, small_in, b2_in = sem("qkvo_in"), sem("small_in"), sem("b2_in")
        x_in = [sem(f"x_in{b}") for b in range(B)]
        x_ready = sem("x_ready")
        masks_ready, pool_step = sem("masks_ready"), sem("pool_step")
        dve_step = sem("dve_step")
        const_pe, const_act, const_dve = sem("const_pe"), sem("const_act"), sem("const_dve")
        zeros_ready, fill_done, tail_filled = sem("zeros_ready"), sem("fill_done"), sem("tail_filled")
        passed = sem("passed")
        var_ready, std_ready, ln_step = sem("var_ready"), sem("std_ready"), sem("ln_step")
        xn_ready, xn_kept = sem("xn_ready"), sem("xn_kept")
        lnT_done, lnT_hi, lnT_lo = sem("lnT_done"), sem("lnT_hi"), sem("lnT_lo")
        logits_done, logits_kept = sem("logits_done"), sem("logits_kept")
        onehot_ready, counts_done = sem("onehot_ready"), sem("counts_done")
        slots_ready, scattered = sem("slots_ready"), sem("scattered")
        w1_in, w2_in, w_split = sem("w1_in"), sem("w2_in"), sem("w_split")
        row_in, rowT_done, rowT_hi, rowT_ready = (sem("row_in"), sem("rowT_done"), sem("rowT_hi"),
                                                  sem("rowT_ready"))
        hid_done, gelu_done, hid_hi, hid_ready = (sem("hid_done"), sem("gelu_done"),
                                                  sem("hid_hi"), sem("hid_ready"))
        y_done, y_biased, y_tanh, g_ready, g_stored = (sem("y_done"), sem("y_biased"),
                                                       sem("y_tanh"), sem("g_ready"),
                                                       sem("g_stored"))
        cur_in = sem("cur_in")
        prep_done, prep_hi, prep_ready = sem("prep_done"), sem("prep_hi"), sem("prep_ready")
        c_ready = sem("c_ready")
        scores_done, acts_done = sem("scores_done"), sem("acts_done")
        mixed, theta_done, exp_done = sem("mixed"), sem("theta_done"), sem("exp_done")
        pT_done, pT_hi0, pT_hi1, pT_ready = (sem("pT_done"), sem("pT_hi0"), sem("pT_hi1"),
                                             sem("pT_ready"))
        pv_done, rden_ready, half_s_ready = sem("pv_done"), sem("rden_ready"), sem("half_s_ready")
        slot_ready = sem("slot_ready")
        g_in = [sem("g_in0"), sem("g_in1")]
        xt_in = [sem("xt_in0"), sem("xt_in1")]
        out_sent = [sem("out_sent0"), sem("out_sent1")]
        scaled, out_ready = sem("scaled"), sem("out_ready")

        wq_raw, wv_raw = sb("wq_raw", [P, DC, D]), sb("wv_raw", [P, DC, D])
        wk_raw = sb("wk_raw", [P, DC, D + 1])
        wo_raw, woT = sb("wo_raw", [P, DC, D]), sb("woT", [P, DC, D])
        bq_wide, bv_wide = sb("bq_wide", [P, DC, P]), sb("bv_wide", [P, DC, P])
        expert_id = sb("expert_id", [P, E, NT])
        keep_scan = sb("keep_scan", [P, E, NT])
        best = sb("best", [P, NT])
        tagged = sb("tagged", [P, E, NT])
        onehot = sb("onehot", [P, E, NT])
        totals = sb("totals", [P, E, NT])
        running = sb("running", [P, E, NT])
        slot_f = sb("slot_f", [P, NT])
        tiles_i = sb("tiles_i", [P, 2, E], I32)
        tiles_f = sb("tiles_f", [P, 3, E])
        with ExitStack() as experts:
            def ex(name, shape, dt=F32):
                return experts.enter_context(nc.sbuf_tensor(name, shape, dt))

            w1_raw, w2_raw = ex("w1_raw", [P, DC, H]), ex("w2_raw", [P, HC, D])
            row = ex("row", [P, D])
            w1_hi = [ex(f"w1_hi{i}", [P, DC, H], F32R) for i in range(2)]
            w1_lo = [ex(f"w1_lo{i}", [P, DC, H], F32R) for i in range(2)]
            w2_hi = [ex(f"w2_hi{i}", [P, HC, D], F32R) for i in range(2)]
            w2_lo = [ex(f"w2_lo{i}", [P, HC, D], F32R) for i in range(2)]
            rowT_h, rowT_l = ex("rowT_h", [P, DC, P], F32R), ex("rowT_l", [P, DC, P], F32R)
            hid = ex("hid", [P, HC, P])
            hid_h, hid_l = ex("hid_h", [P, HC, P], F32R), ex("hid_l", [P, HC, P], F32R)
            y_sb, y_t, g_sb = ex("y_sb", [P, D]), ex("y_t", [P, D]), ex("g_sb", [P, D])

        u_hi, u_lo = sb("u_hi", [P, DC, S], F32R), sb("u_lo", [P, DC, S], F32R)
        v_hi, v_lo = sb("v_hi", [P, TPB, VW], F32R), sb("v_lo", [P, TPB, VW], F32R)
        theta = sb("theta", [P, 2, S])
        tanh_s = sb("tanh_s", [P, S])
        relu_s = sb("relu_s", [P, S])
        neg_max = sb("neg_max", [P, 2, 2])
        pT_hi, pT_lo = sb("pT_hi", [P, TPB, P], F32R), sb("pT_lo", [P, TPB, P], F32R)
        c_cur = sb("c_cur", [P, 2, TPB])
        rden = sb("rden", [P, 2])
        half_s = sb("half_s", [P, 2, D])
        g_tile = sb("g_tile", [P, 2, D])
        x_tile = sb("x_tile", [P, 2, D])
        slot_cur = sb("slot_cur", [P, 2], I32)

        block = ctx.enter_context(nc.Block())

        b1_rows = b1.rearrange("e (c p) -> (e c) p", p=P)
        chunked = lambda w: w.rearrange("(c p) n -> p c n", p=P)
        S_BANK, PT_BANK, O_BANK = 0, 4, 6
        GROUPS = [(0, 4), (4, 6), (6, 8)]
        NG = len(GROUPS)
        HID_BANKS = [0, 1, 2, 3, 5, 7]
        HB = len(HID_BANKS)

        def hid_ps(j):
            return ps[:, HID_BANKS[j % HB], (j // HB) * P:(j // HB + 1) * P]

        JT, JU, JV = 4, 4, TPB
        JOBS = JT + JU + JV
        KA = K_SIGMOID / 2
        KT, KR = K_TANH / KA, K_RELU / KA

        def wait_apart(engine, semaphore, value):
            engine.wait_ge(semaphore, value)
            engine.sem_inc(passed, 1)

        @block.sync
        def _(sp):
            for b in range(B):
                sp.dma_start(xn_all[:, b * TPB:(b + 1) * TPB, :],
                             x_rows[b * S:(b + 1) * S, :].rearrange("(i p) d -> p i d", p=P)
                             ).then_inc(x_in[b], 16)
            sp.wait_ge(zeros_ready, 1)
            sp.dma_start(sorted_x.rearrange("(i p) d -> p i d", p=P),
                         zeros[:, :].rearrange("p (a d) -> p a d", a=1)
                         .to_broadcast([P, MAX_TILES + 1, D])).then_inc(fill_done, 16)
            sp.dma_start(sorted_g[NT * P:, :].rearrange("(i p) d -> p i d", p=P),
                         zeros[:, :].rearrange("p (a d) -> p a d", a=1)
                         .to_broadcast([P, MAX_TILES - NT, D])).then_inc(tail_filled, 16)
            sp.wait_ge(tail_filled, 16)
            sp.sem_inc(g_stored, 16)
            for b in range(B):
                sp.wait_ge(x_in[b], 16)
                sp.sem_inc(x_ready, 1)
            sp.wait_ge(scattered, 16 * NT)
            sp.wait_ge(slots_ready, 1)
            sp.dma_start(row[:, :], sorted_x[0:P, :]).then_inc(row_in, 16)
            with sp.Fori(0, E) as e:
                t0 = sp.value_load(first_tile[0:1, bass.ds(e, 1)], min_val=0, max_val=MAX_TILES - 1)
                t1 = sp.value_load(first_tile[0:1, bass.ds(e + 1, 1)], min_val=1, max_val=MAX_TILES)
                with sp.Fori(t0, t1) as t:
                    sp.wait_ge(rowT_done, t + 1)
                    sp.dma_start(row[:, :], sorted_x[bass.ds(t * P + P, P), :]).then_inc(row_in, 16)
                    sp.wait_ge(g_ready, t + 1)
                    sp.dma_start(sorted_g[bass.ds(t * P, P), :], g_sb[:, :]).then_inc(g_stored, 16)
            sp.wait_ge(xn_kept, B + 1)
            sp.dma_start(xn_cur[:, :, :], xn_all[:, 0:TPB, :]).then_inc(cur_in, 16)
            for j in range(2):
                sp.dma_start(x_tile[:, j, :], x_rows[j * P:(j + 1) * P, :]).then_inc(xt_in[j], 16)

            def batch(b, last):
                if not last:
                    sp.wait_ge(prep_done, b * JOBS + JT)
                    sp.dma_start(xn_cur[:, :, :], xn_all[:, bass.ds(b * TPB + TPB, TPB), :]
                                 ).then_inc(cur_in, 16)
                for j in range(TPB):
                    sp.wait_ge(out_ready, b * TPB + j + 1)
                    sp.dma_start(out_rows[bass.ds(b * S + j * P, P), :], g_tile[:, j % 2, :]
                                 ).then_inc(out_sent[j % 2], 16)
                    if not (last and j + 2 >= TPB):
                        sp.dma_start(x_tile[:, j % 2, :], x_rows[bass.ds(b * S + (j + 2) * P, P), :]
                                     ).then_inc(xt_in[j % 2], 16)

            with sp.Fori(0, B - 1) as b:
                batch(b, False)
            batch(B - 1, True)
            for j in range(2):
                sp.wait_ge(out_sent[j], 16 * NT // 2)

        @block.gpsimd
        def _(pool):
            nc.gpsimd.memset(zeros[:, :], 0.0).then_inc(zeros_ready, 1)
            nc.gpsimd.memset(ident[:, :], 0.0).then_inc(pool_step, 1)
            nc.gpsimd.memset(before[:, :], 1.0).then_inc(pool_step, 1)
            pool.wait_ge(pool_step, 2)
            nc.gpsimd.affine_select(out=ident[:, :], in_=ident[:, :], compare_op=ALU.not_equal, fill=1.0,
                                    base=0, pattern=[[-1, P]], channel_multiplier=1).then_inc(masks_ready, 1)
            nc.gpsimd.affine_select(out=before[:, :], in_=before[:, :], compare_op=ALU.is_gt, fill=0.0,
                                    base=0, pattern=[[1, P]], channel_multiplier=-1).then_inc(masks_ready, 1)
            nc.gpsimd.iota(expert_id[:, :, :], pattern=[[1, E], [0, NT]], base=0, channel_multiplier=0,
                           allow_small_or_imprecise_dtypes=True).then_inc(masks_ready, 1)
            pool.sem_inc(xn_kept, 1)

            with pool.Fori(0, B) as b:
                wait_apart(pool, xn_ready, b + 1)
                nc.gpsimd.tensor_copy(xn_all[:, bass.ds(b * TPB, TPB), :], xn_cur[:, :, :]).then_inc(xn_kept, 1)

            pool.wait_ge(fill_done, 16)
            pool.wait_ge(slots_ready, 1)
            pool.wait_ge(xn_kept, B + 1)
            for i in range(NT):
                pool.indirect_dma_start(sorted_x, bass.IndirectOffsetOnAxis(ap=slot_i[:, i:i + 1], axis=0),
                                        xn_all[:, i, :], None).then_inc(scattered, 16)

            def load_weights(e):
                pool.dma_start(w1_raw[:, :, :], W1[bass.ds(e, 1)].rearrange(
                    "a (c p) n -> p (a c) n", p=P)).then_inc(w1_in, 16)
                pool.dma_start(w2_raw[:, :, :], W2[bass.ds(e, 1)].rearrange(
                    "a (c p) n -> p (a c) n", p=P)).then_inc(w2_in, 16)

            def split_weights(e, par):
                wait_apart(pool, w1_in, e * 16 + 16)
                nc.gpsimd.tensor_copy(w1_hi[par][:, :, :], w1_raw[:, :, :]).then_inc(w_split, 1)
                pool.wait_ge(w_split, e * 4 + 1)
                nc.gpsimd.tensor_tensor(w1_lo[par][:, :, :], w1_raw[:, :, :],
                                        w1_hi[par][:, :, :].bitcast(F32), ALU.subtract).then_inc(w_split, 1)
                wait_apart(pool, w2_in, e * 16 + 16)
                nc.gpsimd.tensor_copy(w2_hi[par][:, :, :], w2_raw[:, :, :]).then_inc(w_split, 1)
                pool.wait_ge(w_split, e * 4 + 3)
                nc.gpsimd.tensor_tensor(w2_lo[par][:, :, :], w2_raw[:, :, :],
                                        w2_hi[par][:, :, :].bitcast(F32), ALU.subtract).then_inc(w_split, 1)

            for e in range(2):
                if e:
                    pool.wait_ge(w_split, e * 4)
                load_weights(e)
                split_weights(e, e)
            with pool.Fori(1, E // 2) as pair:
                for par in range(2):
                    e = pair * 2 + par
                    pool.wait_ge(w_split, e * 4)
                    load_weights(e)
                    tiles = pool.value_load(first_tile[0:1, bass.ds(e - 1, 1)], min_val=1, max_val=MAX_TILES)
                    pool.wait_ge(y_done, tiles)
                    split_weights(e, par)

            total = pool.value_load(first_tile[0:1, E:E + 1], min_val=E, max_val=MAX_TILES)
            wait_apart(pool, g_stored, total * 16 + 16)

            def gather(n, par):
                nc.gpsimd.tensor_copy(slot_cur[:, par:par + 1], slot_i[:, bass.ds(n, 1)]).then_inc(slot_ready, 1)
                wait_apart(pool, slot_ready, n + 1)
                pool.indirect_dma_start(g_tile[:, par, :], None, sorted_g,
                                        bass.IndirectOffsetOnAxis(ap=slot_cur[:, par:par + 1], axis=0)
                                        ).then_inc(g_in[par], 16)

            for n in range(2):
                gather(n, n)
            pool.sem_inc(scaled, 2)

            def batch(b, last):
                for j in range(TPB):
                    n, par = b * TPB + j, j % 2
                    turn = b * (TPB // 2) + j // 2 + 1
                    pool.wait_ge(half_s_ready, n + 1)
                    pool.wait_ge(g_in[par], turn * 16)
                    nc.gpsimd.tensor_tensor(g_tile[:, par, :], half_s[:, par, :], g_tile[:, par, :],
                                            ALU.mult).then_inc(scaled, 1)
                    pool.wait_ge(scaled, n + 3)
                    pool.wait_ge(xt_in[par], turn * 16)
                    nc.gpsimd.tensor_tensor(g_tile[:, par, :], g_tile[:, par, :], x_tile[:, par, :],
                                            ALU.add).then_inc(out_ready, 1)
                    if not (last and j + 2 >= TPB):
                        wait_apart(pool, out_sent[par], turn * 16)
                        gather(n + 2, par)

            with pool.Fori(0, B - 1) as b:
                batch(b, False)
            batch(B - 1, True)

        @block.scalar
        def _(act):
            for dst, src in ((wq_raw, Wq), (wk_raw, Wk), (wv_raw, Wv), (wo_raw, Wo)):
                act.dma_start(dst[:, :, 0:D], chunked(src)).then_inc(qkvo_in, 16)
            act.dma_start(bias_rows[0:E * HC, :], b1_rows).then_inc(small_in, 16)
            for first, src in ((BQ, bq), (BK, bk), (BV, bv)):
                act.dma_start(bias_rows[first:first + DC, :], src.rearrange("(c p) -> c p", p=P)).then_inc(small_in, 16)
            act.dma_start(bo_row[:, :], bo.rearrange("(a d) -> a d", a=1)).then_inc(small_in, 16)
            act.dma_start(br_all[:, :], br.rearrange("(a e) -> a e", a=1).to_broadcast([P, E])).then_inc(small_in, 16)
            act.dma_start(small_w[:, :, 0:E], chunked(Wr)).then_inc(small_in, 16)
            act.dma_start(b2_all[:, :], b2.rearrange("e (a d) -> a (e d)", a=1).to_broadcast([P, E * D])
                          ).then_inc(b2_in, 16)
            act.wait_ge(zeros_ready, 1)
            nc.scalar.activation(warm[:, 0:1], zeros[:, 0:1], ACT.Sqrt)
            act.wait_ge(const_pe, 3)
            for m in range(DC):
                nc.scalar.activation(M_hi[:, m, :], ps[:, 2 + m, 0:D], ACT.Copy)
            nc.scalar.activation(G_hi[:, :, :], ps[:, 5, :].rearrange("p (m d) -> p m d", m=DC), ACT.Copy
                                 ).then_inc(const_act, 1)
            with act.Fori(0, B) as b:
                act.wait_ge(var_ready, b + 1)
                nc.scalar.activation(std[:, :], std[:, :], ACT.Sqrt).then_inc(std_ready, 1)
                for q in range(4):
                    act.wait_ge(lnT_done, b * 4 + q + 1)
                    nc.scalar.activation(xnT_hi[:, q // 2, (q % 2) * HALF:(q % 2 + 1) * HALF], ps[:, q, :],
                                         ACT.Copy).then_inc(lnT_hi, 1)

            def row_high(t):
                act.wait_ge(rowT_done, t + 1)
                nc.scalar.activation(rowT_h[:, :, :], ps[:, 4, 0:D].rearrange("p (c n) -> p c n", c=DC), ACT.Copy
                                     ).then_inc(rowT_hi, 1)

            nc.scalar.activation(warm[:, 1:2], zeros[:, 0:1], ACT.Gelu)
            act.wait_ge(slots_ready, 1)
            row_high(0)
            with act.Fori(0, E) as e:
                t0 = act.value_load(first_tile[0:1, bass.ds(e, 1)], min_val=0, max_val=MAX_TILES - 1)
                t1 = act.value_load(first_tile[0:1, bass.ds(e + 1, 1)], min_val=1, max_val=MAX_TILES)
                with act.Fori(t0, t1) as t:
                    for j in range(HC):
                        act.wait_ge(hid_done, t * HC + j + 1)
                        nc.scalar.activation(hid[:, j, :], hid_ps(j), ACT.Gelu,
                                             bias=bias_cols[:, bass.ds(e * HC + j, 1)]).then_inc(gelu_done, 1)
                    row_high(t + 1)
                    act.wait_ge(y_biased, t + 1)
                    nc.scalar.activation(y_t[:, :], y_sb[:, :], ACT.Tanh, scale=0.5).then_inc(y_tanh, 1)
            nc.scalar.activation(warm[:, 2:3], zeros[:, 0:1], ACT.Exp)

            def high(n_batch, jobs):
                for q in jobs:
                    act.wait_ge(prep_done, n_batch * JOBS + q + 1)
                    if q < JT:
                        nc.scalar.activation(xnT_hi[:, q // 2, (q % 2) * HALF:(q % 2 + 1) * HALF], ps[:, q % 2, :],
                                             ACT.Copy).then_inc(prep_hi, 1)
                    elif q < JT + JU:
                        m, h = divmod(q - JT, 2)
                        nc.scalar.activation(u_hi[:, m, h * HALF:(h + 1) * HALF], ps[:, q % 2, :], ACT.Identity,
                                             bias=r_col[:, m:m + 1]).then_inc(prep_hi, 1)
                    else:
                        nc.scalar.activation(v_hi[:, q - JT - JU, 0:D], ps[:, q % 2, 0:D], ACT.Copy
                                             ).then_inc(prep_hi, 1)

            def tanhs(n, j, h):
                bank, cols = ps[:, S_BANK + 2 * (j % 2) + h, :], slice(h * HALF, (h + 1) * HALF)
                act.wait_ge(scores_done, n * 2 + h + 1)
                nc.scalar.activation(theta[:, j % 2, cols], bank, ACT.Tanh, bias=c_cur[:, 1, j:j + 1], scale=0.5)
                nc.scalar.activation(tanh_s[:, cols], bank, ACT.Tanh, bias=c_cur[:, 0, j:j + 1])

            def relu(j, h):
                nc.scalar.activation(relu_s[:, h * HALF:(h + 1) * HALF], ps[:, S_BANK + 2 * (j % 2) + h, :], ACT.Relu,
                                     bias=c_cur[:, 0, j:j + 1], scale=KR).then_inc(acts_done, 1)

            def exps(n, j):
                act.wait_ge(theta_done, n + 1)
                for h in range(2):
                    part = theta[:, j % 2, h * HALF:(h + 1) * HALF]
                    nc.scalar.activation(part, part, ACT.Exp, bias=neg_max[:, j % 2, 1:2], scale=-1.0
                                         ).then_inc(exp_done, 1)

            assert KR == 1.0

            def first_tile_acts(nb):
                act.wait_ge(c_ready, nb + 1)
                for h in range(2):
                    tanhs(nb * TPB, 0, h)
                    relu(0, h)

            def batch(b, last):
                for j in range(TPB):
                    n = b * TPB + j
                    if j + 1 < TPB:
                        tanhs(n + 1, j + 1, 0)
                    elif not last:
                        high(b + 1, range(0, JT))
                    act.wait_ge(pT_done, n * 2 + 2)
                    nc.scalar.activation(pT_hi[:, TPB // 2:, :], ps[:, PT_BANK + 1, :].rearrange(
                        "p (c n) -> p c n", n=P), ACT.Copy).then_inc(pT_hi1, 1)
                    if j + 1 < TPB:
                        relu(j + 1, 0)
                        tanhs(n + 1, j + 1, 1)
                        relu(j + 1, 1)
                        exps(n + 1, j + 1)
                    elif not last:
                        high(b + 1, range(JT, JOBS))
                        first_tile_acts(b + 1)
                        exps(n + 1, 0)

            high(0, range(JOBS))
            first_tile_acts(0)
            exps(0, 0)
            with act.Fori(0, B - 1) as b:
                batch(b, False)
            batch(B - 1, True)

        @block.tensor
        def _(pe):
            mm = nc.tensor.matmul

            def product(dst, a_hi, a_lo, b_hi, b_lo, first, last):
                mm(dst, a_hi, b_hi, start=first, stop=False)
                mm(dst, a_hi, b_lo, start=False, stop=False)
                return mm(dst, a_lo, b_hi, start=False, stop=last)

            pe.wait_ge(masks_ready, 1)
            pe.wait_ge(small_in, 16 * 7)
            nr = E * HC + 3 * DC
            nc.tensor.transpose(ps[:, 0, 0:nr], bias_rows[:, :], ident[0:nr, 0:nr]).then_inc(const_pe, 1)
            pe.wait_ge(qkvo_in, 16 * 4)
            for ec in range(DC):
                for fc in range(DC):
                    last = nc.tensor.transpose(ps[:, 1, ec * D + fc * P:ec * D + (fc + 1) * P],
                                               wo_raw[:, fc, ec * P:(ec + 1) * P], ident[:, :])
            last.then_inc(const_pe, 1)
            pe.wait_ge(const_dve, 1)
            for m in range(DC):
                for ec in range(DC):
                    mm(ps[:, 2 + m, 0:D + 1], wq_raw[:, ec, m * P:(m + 1) * P], wk_raw[:, ec, :],
                       start=ec == 0, stop=ec == DC - 1)
            for m in range(DC):
                for ec in range(DC):
                    mm(ps[:, 4, m:m + 1], wk_raw[:, ec, m * P:(m + 1) * P], bias_cols[:, BQ + ec:BQ + ec + 1],
                       start=ec == 0, stop=ec == DC - 1)
            for ec in range(DC):
                mm(ps[:, 4, DC:DC + 1], bq_wide[:, ec, :], bias_cols[:, BK + ec:BK + ec + 1],
                   start=ec == 0, stop=ec == DC - 1)
            for m in range(DC):
                for ec in range(DC):
                    mm(ps[:, 5, m * D:(m + 1) * D], wv_raw[:, ec, m * P:(m + 1) * P], woT[:, ec, :],
                       start=ec == 0, stop=ec == DC - 1)
            for ec in range(DC):
                mm(ps[:, 6, 0:D], bv_wide[:, ec, :], woT[:, ec, :], start=ec == 0, stop=False)
            mm(ps[:, 6, 0:D], ones[0:1, :], bo_row[:, :], start=False, stop=True).then_inc(const_pe, 1)

            pe.wait_ge(const_dve, 2)
            with pe.Fori(0, B) as b:
                pe.wait_ge(xn_ready, b + 1)
                for q in range(4):
                    k, i0 = q // 2, (q % 2) * 4
                    for i in range(4):
                        last = nc.tensor.transpose(ps[:, q, i * P:(i + 1) * P],
                                                   xn_cur[:, i0 + i, k * P:(k + 1) * P], ident[:, :])
                    last.then_inc(lnT_done, 1)
                pe.wait_ge(lnT_lo, b * 4 + 4)
                for i in range(TPB):
                    for k in range(DC):
                        cols = slice(i * P, (i + 1) * P)
                        last = product(ps[:, 4, i * SM:(i + 1) * SM], xnT_hi[:, k, cols], xnT_lo[:, k, cols],
                                       R_hi[:, k, :], R_lo[:, k, :], k == 0, k == DC - 1)
                last.then_inc(logits_done, 1)
            pe.wait_ge(onehot_ready, 1)
            pe.wait_ge(masks_ready, 3)
            oh = onehot[:, :, :].rearrange("p e i -> p (e i)")
            mm(ps[:, 5, 0:E * NT], before[:, :], oh, start=True, stop=True)
            mm(ps[:, 6, 0:E * NT], ones[:, :], oh, start=True, stop=True).then_inc(counts_done, 1)

            def turn_row(t):
                pe.wait_ge(row_in, t * 16 + 16)
                for k in range(DC):
                    last = nc.tensor.transpose(ps[:, 4, k * P:(k + 1) * P], row[:, k * P:(k + 1) * P], ident[:, :])
                last.then_inc(rowT_done, 1)

            pe.wait_ge(slots_ready, 1)
            turn_row(0)
            with pe.Fori(0, E // 2) as pair:
                for par in range(2):
                    e = pair * 2 + par
                    t0 = pe.value_load(first_tile[0:1, bass.ds(e, 1)], min_val=0, max_val=MAX_TILES - 1)
                    t1 = pe.value_load(first_tile[0:1, bass.ds(e + 1, 1)], min_val=1, max_val=MAX_TILES)
                    with pe.Fori(t0, t1) as t:
                        pe.wait_ge(w_split, e * 4 + 4)
                        pe.wait_ge(rowT_ready, t + 1)
                        for j in range(HC):
                            if j >= HB:
                                pe.wait_ge(gelu_done, t * HC + j - HB + 1)
                            for k in range(DC):
                                cols = slice(j * P, (j + 1) * P)
                                last = product(hid_ps(j),
                                               w1_hi[par][:, k, cols], w1_lo[par][:, k, cols],
                                               rowT_h[:, k, :], rowT_l[:, k, :], k == 0, k == DC - 1)
                            last.then_inc(hid_done, 1)
                        turn_row(t + 1)
                        for g, (j0, j1) in enumerate(GROUPS):
                            pe.wait_ge(hid_ready, t * NG + g + 1)
                            for j in range(j0, j1):
                                last = product(ps[:, 6, 0:D], hid_h[:, j, :], hid_l[:, j, :],
                                               w2_hi[par][:, j, :], w2_lo[par][:, j, :], j == 0, j == HC - 1)
                        last.then_inc(y_done, 1)

            def prepare(nb, jobs):
                for q in jobs:
                    if q == 0:
                        pe.wait_ge(cur_in, nb * 16 + 16)
                    if q >= 2:
                        pe.wait_ge(prep_ready, nb * JOBS + (max(q - 1, JT) if q >= JT else q - 1))
                    bank = ps[:, S_BANK + q % 2, :]
                    if q < JT:
                        k, i0 = q // 2, (q % 2) * 4
                        for i in range(4):
                            last = nc.tensor.transpose(bank[:, i * P:(i + 1) * P],
                                                       xn_cur[:, i0 + i, k * P:(k + 1) * P], ident[:, :])
                    elif q < JT + JU:
                        m, h = divmod(q - JT, 2)
                        for k in range(DC):
                            rows, cols = slice(m * P, (m + 1) * P), slice(h * HALF, (h + 1) * HALF)
                            last = product(bank, M_hi[:, k, rows], M_lo[:, k, rows],
                                           xnT_hi[:, k, cols], xnT_lo[:, k, cols], k == 0, k == DC - 1)
                    else:
                        i = q - JT - JU
                        for k in range(DC):
                            cols = slice(i * P, (i + 1) * P)
                            last = product(bank[:, 0:D], xnT_hi[:, k, cols], xnT_lo[:, k, cols],
                                           G_hi[:, k, :], G_lo[:, k, :], k == 0, k == DC - 1)
                    last.then_inc(prep_done, 1)

            def scores(n, j, h):
                for k in range(DC):
                    rows, cols = slice(j * P, (j + 1) * P), slice(h * HALF, (h + 1) * HALF)
                    last = product(ps[:, S_BANK + 2 * (j % 2) + h, :], u_hi[:, k, rows], u_lo[:, k, rows],
                                   xnT_hi[:, k, cols], xnT_lo[:, k, cols], k == 0, k == DC - 1)
                last.then_inc(scores_done, 1)

            def first_scores(nb):
                pe.wait_ge(prep_ready, nb * JOBS + JOBS)
                for h in range(2):
                    scores(nb * TPB, 0, h)

            def batch(b, last_batch):
                for j in range(TPB):
                    n = b * TPB + j
                    if j + 1 < TPB:
                        scores(n + 1, j + 1, 0)
                    elif not last_batch:
                        prepare(b + 1, range(0, JT))
                    for h in range(2):
                        pe.wait_ge(exp_done, n * 2 + h + 1)
                        for i in range(4):
                            last = nc.tensor.transpose(
                                ps[:, PT_BANK + h, i * P:(i + 1) * P],
                                theta[:, j % 2, h * HALF + i * P:h * HALF + (i + 1) * P], ident[:, :])
                        last.then_inc(pT_done, 1)
                    if j + 1 < TPB:
                        scores(n + 1, j + 1, 1)
                    elif not last_batch:
                        prepare(b + 1, range(JT, JT + JU))
                    for i in range(TPB):
                        if i % 4 == 0:
                            pe.wait_ge(pT_ready, n * 2 + i // 4 + 1)
                        last = product(ps[:, O_BANK + j % 2, 0:VW], pT_hi[:, i, :], pT_lo[:, i, :],
                                       v_hi[:, i, :], v_lo[:, i, :], i == 0, i == TPB - 1)
                    last.then_inc(pv_done, 1)
                if not last_batch:
                    prepare(b + 1, range(JT + JU, JOBS))
                    first_scores(b + 1)

            prepare(0, range(JOBS))
            first_scores(0)
            with pe.Fori(0, B - 1) as b:
                batch(b, False)
            batch(B - 1, True)

        @block.vector
        def _(dve):
            v = nc.vector
            steps = [0]

            def step(ins):
                steps[0] += 1
                ins.then_inc(dve_step, 1)
                dve.wait_ge(dve_step, steps[0])

            v.memset(ones[:, :], 1.0)
            v.memset(keep_scan[:, :, :], 1.0)
            step(v.memset(small_w[:, :, E + 1:SM], 0.0))
            step(v.memset(keep_scan[:, :, 0:1], 0.0))
            dve.wait_ge(const_pe, 1)
            step(v.tensor_copy(bias_cols[:, :], ps[:, 0, 0:E * HC + 3 * DC]))
            dve.wait_ge(qkvo_in, 16 * 4)
            for ec in range(DC):
                v.tensor_copy(wk_raw[:, ec, D:D + 1], bias_cols[:, BK + ec:BK + ec + 1])
                v.tensor_scalar(bq_wide[:, ec, :], ones[:, :], bias_cols[:, BQ + ec:BQ + ec + 1], None, ALU.mult)
                v.tensor_scalar(bv_wide[:, ec, :], ones[:, :], bias_cols[:, BV + ec:BV + ec + 1], None, ALU.mult)
            dve.wait_ge(const_pe, 2)
            v.tensor_copy(woT[:, :, :], ps[:, 1, :].rearrange("p (c f) -> p c f", c=DC)).then_inc(const_dve, 1)
            dve.wait_ge(const_pe, 3)
            dve.wait_ge(const_act, 1)
            dve.wait_ge(small_in, 16 * 7)
            for m in range(DC):
                v.tensor_copy(small_w[:, m, E:E + 1], ps[:, 2 + m, D:D + 1])
            v.tensor_copy(r_col[:, :], ps[:, 4, 0:DC])
            v.tensor_copy(kappa[:, :], ps[:, 4, DC:DC + 1])
            step(v.tensor_scalar(attn_const[:, :], ps[:, 6, 0:D], 0.5, None, ALU.mult))
            step(v.tensor_copy(R_hi[:, :, :], small_w[:, :, :]))
            v.tensor_tensor(R_lo[:, :, :], small_w[:, :, :], R_hi[:, :, :].bitcast(F32), ALU.subtract)
            for m in range(DC):
                v.tensor_tensor(M_lo[:, m, :], ps[:, 2 + m, 0:D], M_hi[:, m, :].bitcast(F32), ALU.subtract)
            v.tensor_tensor(G_lo[:, :, :], ps[:, 5, :].rearrange("p (m d) -> p m d", m=DC),
                            G_hi[:, :, :].bitcast(F32), ALU.subtract).then_inc(const_dve, 1)

            LN_STEPS = 3
            with dve.Fori(0, B) as b:
                dve.wait_ge(x_ready, b + 1)
                for i in range(TPB):
                    last = v.bn_stats(stats[:, i, :], xn_all[:, bass.ds(b * TPB + i, 1), :])
                last.then_inc(ln_step, 1)
                wait_apart(dve, ln_step, b * LN_STEPS + 1)
                for i in range(TPB):
                    last = v.bn_aggr(mean_var[:, i, :], stats[:, i, :])
                last.then_inc(ln_step, 1)
                dve.wait_ge(ln_step, b * LN_STEPS + 2)
                v.tensor_scalar(std[:, :], mean_var[:, :, 1], LN_EPS, None, ALU.add).then_inc(var_ready, 1)
                dve.wait_ge(std_ready, b + 1)
                v.reciprocal(rstd[:, :], std[:, :]).then_inc(ln_step, 1)
                dve.wait_ge(ln_step, b * LN_STEPS + 3)
                dve.wait_ge(xn_kept, b + 1)
                for i in range(TPB):
                    last = v.tensor_scalar(xn_cur[:, i, :], xn_all[:, bass.ds(b * TPB + i, 1), :],
                                           mean_var[:, i, 0:1], rstd[:, i:i + 1], ALU.subtract, ALU.mult)
                last.then_inc(xn_ready, 1)
                for q in range(4):
                    cols = slice((q % 2) * HALF, (q % 2 + 1) * HALF)
                    dve.wait_ge(lnT_hi, b * 4 + q + 1)
                    v.tensor_tensor(xnT_lo[:, q // 2, cols], ps[:, q, :], xnT_hi[:, q // 2, cols].bitcast(F32),
                                    ALU.subtract).then_inc(lnT_lo, 1)
                dve.wait_ge(logits_done, b + 1)
                small = ps[:, 4, 0:TPB * SM].rearrange("p (i s) -> p i s", s=SM)
                v.tensor_tensor(logits[:, :, bass.ds(b * TPB, TPB)].rearrange("p e i -> p i e"), small[:, :, 0:E],
                                br_all[:, :].rearrange("p (a e) -> p a e", a=1).to_broadcast([P, TPB, E]), ALU.add)
                v.tensor_scalar(c_all[:, bass.ds(b * TPB, TPB)], small[:, :, E], kappa[:, 0:1], None, ALU.add
                                ).then_inc(logits_kept, 1)

            dve.wait_ge(logits_kept, B)
            dve.wait_ge(masks_ready, 3)
            by_token = lambda a: a[:, :, :].rearrange("p e i -> p i e")
            over_experts = lambda a: a[:, :].rearrange("p (a i) -> p a i", a=1).to_broadcast([P, E, NT])
            over_tiles = lambda a: a.rearrange("p (e a) -> p e a", a=1).to_broadcast([P, E, NT])
            step(v.tensor_reduce(best[:, :], by_token(logits), X, ALU.max))
            step(v.tensor_tensor(onehot[:, :, :], logits[:, :, :], over_experts(best), ALU.is_ge))
            step(v.scalar_tensor_tensor(tagged[:, :, :].rearrange("p e i -> p (e i)"),
                                        onehot[:, :, :].rearrange("p e i -> p (e i)"), float(-E),
                                        expert_id[:, :, :].rearrange("p e i -> p (e i)"), ALU.mult, ALU.add))
            step(v.tensor_reduce(best[:, :], by_token(tagged), X, ALU.min))
            v.tensor_tensor(onehot[:, :, :], tagged[:, :, :], over_experts(best), ALU.is_equal
                            ).then_inc(onehot_ready, 1)
            dve.wait_ge(counts_done, 1)
            flat = lambda a: a[:, :, :].rearrange("p e i -> p (e i)")
            step(v.tensor_copy(flat(totals), ps[:, 6, 0:E * NT]))
            step(v.tensor_tensor_scan(flat(running), flat(keep_scan), flat(totals), 0.0, ALU.mult, ALU.add))
            step(v.tensor_scalar(tiles_i[:, 0, :], running[:, :, NT - 1], float(P - 1), None, ALU.add))
            step(v.tensor_scalar(tiles_i[:, 1, :], tiles_i[:, 0, :], 7, None, ALU.arith_shift_right))
            step(v.tensor_scalar(tiles_f[:, 0, :], tiles_i[:, 1, :], 1.0, None, ALU.max))
            step(v.tensor_tensor_scan(tiles_f[:, 1, :], ones[:, 0:E], tiles_f[:, 0, :], 0.0, ALU.mult, ALU.add))
            v.memset(first_tile[:, 0:1], 0)
            v.tensor_copy(first_tile[:, 1:E + 1], tiles_f[:, 1, :])
            step(v.tensor_tensor(tiles_f[:, 2, :], tiles_f[:, 1, :], tiles_f[:, 0, :], ALU.subtract))
            step(v.tensor_tensor(running[:, :, :], running[:, :, :], totals[:, :, :], ALU.subtract))
            step(v.tensor_tensor(flat(running), flat(running), ps[:, 5, 0:E * NT], ALU.add))
            step(v.tensor_scalar(tiles_f[:, 2, :], tiles_f[:, 2, :], float(P), None, ALU.mult))
            step(v.tensor_tensor(running[:, :, :], running[:, :, :], over_tiles(tiles_f[:, 2, :]), ALU.add))
            step(v.tensor_tensor(running[:, :, :], running[:, :, :], onehot[:, :, :], ALU.mult))
            step(v.tensor_reduce(slot_f[:, :], by_token(running), X, ALU.add))
            v.tensor_copy(slot_i[:, :], slot_f[:, :]).then_inc(slots_ready, 1)
            dve.wait_ge(slots_ready, 1)

            def row_low(t):
                dve.wait_ge(rowT_hi, t + 1)
                v.tensor_tensor(rowT_l[:, :, :], ps[:, 4, 0:D].rearrange("p (c n) -> p c n", c=DC),
                                rowT_h[:, :, :].bitcast(F32), ALU.subtract).then_inc(rowT_ready, 1)

            dve.wait_ge(b2_in, 16)
            row_low(0)
            with dve.Fori(0, E) as e:
                t0 = dve.value_load(first_tile[0:1, bass.ds(e, 1)], min_val=0, max_val=MAX_TILES - 1)
                t1 = dve.value_load(first_tile[0:1, bass.ds(e + 1, 1)], min_val=1, max_val=MAX_TILES)
                with dve.Fori(t0, t1) as t:
                    for g, (j0, j1) in enumerate(GROUPS):
                        dve.wait_ge(gelu_done, t * HC + j1)
                        v.tensor_copy(hid_h[:, j0:j1, :], hid[:, j0:j1, :]).then_inc(hid_hi, 1)
                        dve.wait_ge(hid_hi, t * NG + g + 1)
                        v.tensor_tensor(hid_l[:, j0:j1, :], hid[:, j0:j1, :], hid_h[:, j0:j1, :].bitcast(F32),
                                        ALU.subtract).then_inc(hid_ready, 1)
                    row_low(t + 1)
                    dve.wait_ge(y_done, t + 1)
                    v.tensor_tensor(y_sb[:, :], ps[:, 6, 0:D], b2_all[:, bass.ds(e * D, D)], ALU.add
                                    ).then_inc(y_biased, 1)
                    dve.wait_ge(y_tanh, t + 1)
                    dve.wait_ge(g_stored, t * 16 + 16)
                    v.scalar_tensor_tensor(g_sb[:, :], y_t[:, :], 1.0, y_sb[:, :], ALU.add, ALU.mult
                                           ).then_inc(g_ready, 1)

            def low(nb, jobs):
                for q in jobs:
                    dve.wait_ge(prep_hi, nb * JOBS + q + 1)
                    if q < JT:
                        cols = slice((q % 2) * HALF, (q % 2 + 1) * HALF)
                        v.tensor_tensor(xnT_lo[:, q // 2, cols], ps[:, q % 2, :], xnT_hi[:, q // 2, cols].bitcast(F32),
                                        ALU.subtract).then_inc(prep_ready, 1)
                    elif q < JT + JU:
                        m, h = divmod(q - JT, 2)
                        cols = slice(h * HALF, (h + 1) * HALF)
                        v.scalar_tensor_tensor(u_lo[:, m, cols], ps[:, q % 2, :], r_col[:, m:m + 1],
                                               u_hi[:, m, cols].bitcast(F32), ALU.add, ALU.subtract
                                               ).then_inc(prep_ready, 1)
                    else:
                        i = q - JT - JU
                        v.tensor_tensor(v_lo[:, i, 0:D], ps[:, q % 2, 0:D], v_hi[:, i, 0:D].bitcast(F32),
                                        ALU.subtract).then_inc(prep_ready, 1)

            def batch_c(nb):
                v.tensor_copy(c_cur[:, 0, :], c_all[:, bass.ds(nb * TPB, TPB)])
                v.tensor_scalar(c_cur[:, 1, :], c_all[:, bass.ds(nb * TPB, TPB)], 0.5, None, ALU.mult
                                ).then_inc(c_ready, 1)

            def thetas(n, j):
                for h in range(2):
                    cols = slice(h * HALF, (h + 1) * HALF)
                    part = theta[:, j % 2, cols]
                    dve.wait_ge(acts_done, n * 2 + h + 1)
                    v.scalar_tensor_tensor(part, tanh_s[:, cols], KT, part, ALU.mult, ALU.add).then_inc(mixed, 1)
                    wait_apart(dve, mixed, n * 3 + 2 * h + 1)
                    least = neg_max[:, j % 2, h:h + 1]
                    ins = v.tensor_tensor_reduce(out=part, in0=part, in1=relu_s[:, cols], scale=-KA,
                                                 scalar=3.0e38 if h == 0 else neg_max[:, j % 2, 0:1],
                                                 op0=ALU.add, op1=ALU.min, accum_out=least)
                    ins.then_inc(mixed if h == 0 else theta_done, 1)
                    if h == 0:
                        wait_apart(dve, mixed, n * 3 + 2)

            def finish(n, j):
                dve.wait_ge(pv_done, n + 1)
                v.reciprocal(rden[:, j % 2:j % 2 + 1], ps[:, O_BANK + j % 2, D:D + 1]).then_inc(rden_ready, 1)
                dve.wait_ge(rden_ready, n + 1)
                dve.wait_ge(scaled, n + 1)
                v.scalar_tensor_tensor(half_s[:, j % 2, :], ps[:, O_BANK + j % 2, 0:D], rden[:, j % 2:j % 2 + 1], attn_const[:, :],
                                       ALU.mult, ALU.add).then_inc(half_s_ready, 1)

            def batch(b, last):
                for j in range(TPB):
                    n = b * TPB + j
                    if j == TPB - 1 and not last:
                        low(b + 1, range(0, JT))
                    dve.wait_ge(pT_done, n * 2 + 1)
                    bank = [ps[:, PT_BANK + h, :].rearrange("p (c n) -> p c n", n=P) for h in range(2)]
                    v.tensor_copy(pT_hi[:, 0:4, :], bank[0]).then_inc(pT_hi0, 1)
                    dve.wait_ge(pT_hi0, n + 1)
                    v.tensor_tensor(pT_lo[:, 0:4, :], bank[0], pT_hi[:, 0:4, :].bitcast(F32), ALU.subtract
                                    ).then_inc(pT_ready, 1)
                    dve.wait_ge(pT_hi1, n + 1)
                    v.tensor_tensor(pT_lo[:, 4:8, :], bank[1], pT_hi[:, 4:8, :].bitcast(F32), ALU.subtract
                                    ).then_inc(pT_ready, 1)
                    if j:
                        finish(n - 1, j - 1)
                    if j + 1 < TPB:
                        thetas(n + 1, j + 1)
                    elif not last:
                        low(b + 1, range(JT, JT + JU))
                finish(n, TPB - 1)
                if not last:
                    low(b + 1, range(JT + JU, JOBS))
                    batch_c(b + 1)
                    thetas(n + 1, 0)

            v.memset(v_hi[:, :, D:D + 1].bitcast(F32), 2.0)
            v.memset(v_hi[:, :, D + 1:VW].bitcast(F32), 0.0)
            v.memset(v_lo[:, :, D:VW].bitcast(F32), 0.0)
            batch_c(0)
            low(0, range(JOBS))
            thetas(0, 0)
            with dve.Fori(0, B - 1) as b:
                batch(b, False)
            batch(B - 1, True)


_INS = ['L0_attn_x', 'L0_attn_Wq', 'L0_attn_bq', 'L0_attn_Wk', 'L0_attn_bk', 'L0_attn_Wv', 'L0_attn_bv', 'L0_attn_Wo',
        'L0_attn_bo', 'L0_ffn_Wr', 'L0_ffn_br', 'L0_ffn_W1', 'L0_ffn_b1', 'L0_ffn_W2', 'L0_ffn_b2']


def kernel(**inputs):
    import numpy as _np
    import concourse.bacc as _bacc
    from concourse import mybir as _mybir
    from concourse.bass_utils import run_bass_kernel_spmd as _run

    nc = _bacc.Bacc("TRN2", target_bir_lowering=False, num_devices=1)
    arrays, args = {}, []
    for name in _INS:
        a = _np.ascontiguousarray(inputs[name])
        arrays[f"in_{name}_dram"] = a
        args.append(nc.dram_tensor(f"in_{name}_dram", a.shape, _mybir.dt.from_np(a.dtype), kind="ExternalInput").ap())
    shape = tuple(inputs['L0_attn_x'].shape)
    args.append(nc.dram_tensor("out_0_dram", shape, F32, kind="ExternalOutput").ap())
    block_attention_moe(nc, *args)
    r = _run(nc, [arrays], core_ids=[0])
    return r.results[0]["out_0_dram"]
```

```python
from contextlib import ExitStack

import concourse.bass as bass
from concourse import mybir

P = 128
F32 = mybir.dt.float32
F32R = mybir.dt.float32r
I32 = mybir.dt.int32
ALU = mybir.AluOpType
ACT = mybir.ActivationFunctionType
X = mybir.AxisListType.X

LN_EPS = 1e-5
BASE_THETA, K_SIGMOID, K_TANH, K_RELU = 0.5, 0.2, 0.15, 0.1


def block_attention_moe(nc, x, Wq, bq, Wk, bk, Wv, bv, Wo, bo, Wr, br, W1, b1, W2, b2, out):
    B, S, D = x.shape
    E, _, H = W1.shape
    DC = D // P
    HC = H // P
    TPB = S // P
    NT = B * TPB
    MAX_TILES = NT + E - 1
    HALF = S // 2
    AHEAD = 2
    TABLE = MAX_TILES + AHEAD
    SM = E + 2
    VW = D + 2
    assert (P, DC, HALF) == (128, 2, 512) and TPB == 8

    x_rows = x.rearrange("b s d -> (b s) d")
    out_rows = out.rearrange("b s d -> (b s) d")
    REGION = (NT + 1) * P
    sorted_x = nc.dram_tensor("sorted_x", (E * REGION, D), F32, kind="Internal").ap()
    sorted_g = nc.dram_tensor("sorted_g", (MAX_TILES * P, D), F32, kind="Internal").ap()

    with ExitStack() as ctx:
        def sb(name, shape, dt=F32):
            return ctx.enter_context(nc.sbuf_tensor(name, shape, dt))

        def sem(name):
            return ctx.enter_context(nc.semaphore(name))

        ps = ctx.enter_context(nc.psum_tensor("ps", [P, 8, 512], F32))

        ident = sb("ident", [P, P])
        before = sb("before", [P, P])
        ones = sb("ones", [P, P])
        zeros = sb("zeros", [P, D])
        warm = sb("warm", [P, 3])
        bias_rows = sb("bias_rows", [3 * DC, P])
        bias_cols = sb("bias_cols", [P, 3 * DC])
        BQ, BK, BV = 0, DC, 2 * DC
        bo_row = sb("bo_row", [1, D])
        br_all = sb("br_all", [P, E])
        b2_all = sb("b2_all", [P, E * D])
        kappa = sb("kappa", [P, 1])
        r_col = sb("r_col", [P, DC])
        attn_const = sb("attn_const", [P, D])
        M_hi, M_lo = sb("M_hi", [P, DC, D], F32R), sb("M_lo", [P, DC, D], F32R)
        G_hi, G_lo = sb("G_hi", [P, DC, D], F32R), sb("G_lo", [P, DC, D], F32R)
        R_parts = sb("R_parts", [P, DC, 2, SM], F32R)
        small_w = sb("small_w", [P, DC, SM])
        xn_all = sb("xn_all", [P, NT, D])
        xn_cur = sb("xn_cur", [P, TPB, D])
        xnT_hi, xnT_lo = sb("xnT_hi", [P, DC, S], F32R), sb("xnT_lo", [P, DC, S], F32R)
        stats = sb("stats", [P, TPB, 6])
        mean_var = sb("mean_var", [P, TPB, 2])
        std = sb("std", [P, TPB])
        rstd = sb("rstd", [P, TPB])
        c_all = sb("c_all", [P, NT])
        slot_i = sb("slot_i", [P, NT], I32)
        slot_g = sb("slot_g", [P, NT], I32)
        first_tile = sb("first_tile", [P, E + 1], I32)
        last_tile = sb("last_tile", [P, E], I32)
        zero_row = sb("zero_row", [P, E], I32)
        tile_row = sb("tile_row", [P, TABLE], I32)
        qkvo_in, small_in, router_in, b2_in = sem("qkvo_in"), sem("small_in"), sem("router_in"), sem("b2_in")
        x_in = [sem(f"x_in{b}") for b in range(B)]
        x_ready = sem("x_ready")
        masks_ready, pool_step = sem("masks_ready"), sem("pool_step")
        dve_step = sem("dve_step")
        const_pe, const_act, const_dve = sem("const_pe"), sem("const_act"), sem("const_dve")
        zeros_ready, filled, tail_filled = sem("zeros_ready"), sem("filled"), sem("tail_filled")
        passed = sem("passed")
        var_ready, std_ready, ln_step = sem("var_ready"), sem("std_ready"), sem("ln_step")
        xn_ready, xn_kept = sem("xn_ready"), sem("xn_kept")
        lnT_done, lnT_hi, lnT_lo = sem("lnT_done"), sem("lnT_hi"), sem("lnT_lo")
        logits_done, sort_step = sem("logits_done"), sem("sort_step")
        onehot_ready, ranks_done = sem("onehot_ready"), sem("ranks_done")
        carry_ready, counts_done = sem("carry_ready"), sem("counts_done")
        slots_ready, zero_rows_ready = sem("slots_ready"), sem("zero_rows_ready")
        tables_ready, slot_g_ready = sem("tables_ready"), sem("slot_g_ready")
        scattered = sem("scattered")
        w1_in, w2_in, b1_in, b1_ready = sem("w1_in"), sem("w2_in"), sem("b1_in"), sem("b1_ready")
        w1_high, w2_high = sem("w1_high"), sem("w2_high")
        w1_split, w2_split = sem("w1_split"), sem("w2_split")
        row_in, rowT_done, rowT_hi, rowT_ready = (sem("row_in"), sem("rowT_done"), sem("rowT_hi"),
                                                  sem("rowT_ready"))
        hid_done, hid_biased, gelu_done = sem("hid_done"), sem("hid_biased"), sem("gelu_done")
        hidT_done, hidT_hi0, hidT_hi1, hidT_ready = (sem("hidT_done"), sem("hidT_hi0"), sem("hidT_hi1"),
                                                     sem("hidT_ready"))
        y_done, y_biased, y_tanh, g_ready, g_stored = (sem("y_done"), sem("y_biased"),
                                                       sem("y_tanh"), sem("g_ready"),
                                                       sem("g_stored"))
        cur_in = sem("cur_in")
        prep_done, prep_hi, prep_ready = sem("prep_done"), sem("prep_hi"), sem("prep_ready")
        c_ready = sem("c_ready")
        scores_done, tanhs_done, acts_done = sem("scores_done"), sem("tanhs_done"), sem("acts_done")
        mixed, theta_done, exp_done = sem("mixed"), sem("theta_done"), sem("exp_done")
        pT_done, pT_hi0, pT_hi1, pT_ready = (sem("pT_done"), sem("pT_hi0"), sem("pT_hi1"),
                                             sem("pT_ready"))
        pv_done, rden_ready, half_s_ready = sem("pv_done"), sem("rden_ready"), sem("half_s_ready")
        slot_ready = sem("slot_ready")
        g_in = [sem("g_in0"), sem("g_in1")]
        xt_in = [sem("xt_in0"), sem("xt_in1")]
        out_sent = [sem("out_sent0"), sem("out_sent1")]
        scaled, out_ready = sem("scaled"), sem("out_ready")

        wq_raw, wv_raw = sb("wq_raw", [P, DC, D]), sb("wv_raw", [P, DC, D])
        wk_raw = sb("wk_raw", [P, DC, D + 1])
        wo_raw, woT = sb("wo_raw", [P, DC, D]), sb("woT", [P, DC, D])
        bq_wide, bv_wide = sb("bq_wide", [P, DC, P]), sb("bv_wide", [P, DC, P])
        expert_id = sb("expert_id", [P, E, NT])
        tile_id = sb("tile_id", [P, TABLE])
        keep_scan = sb("keep_scan", [P, E, TPB + 1])
        logits = sb("logits", [P, 2, E, TPB])
        best = sb("best", [P, TPB])
        tagged = sb("tagged", [P, E, TPB])
        onehot = sb("onehot", [P, E, TPB + 1])
        running = sb("running", [P, E, TPB + 1])
        rank = sb("rank", [P, E, TPB])
        rank_all = sb("rank_all", [P, NT])
        tag_all = sb("tag_all", [P, NT])
        slot_f = sb("slot_f", [P, TPB])
        tiles_i = sb("tiles_i", [P, 2, E], I32)
        tiles_f = sb("tiles_f", [P, 3, E])
        gap = sb("gap", [P, E])
        last_used = sb("last_used", [P, 1])
        used_tile = sb("used_tile", [P, TABLE])
        after = sb("after", [P, E, TABLE])
        skipped = sb("skipped", [P, TABLE])
        chosen = sb("chosen", [P, E, NT])
        first_slot = sb("first_slot", [P, NT])
        with ExitStack() as experts:
            def ex(name, shape, dt=F32):
                return experts.enter_context(nc.sbuf_tensor(name, shape, dt))

            w1_raw, w2_raw = ex("w1_raw", [P, DC, H]), ex("w2_raw", [P, HC, D])
            row = ex("row", [P, D])
            w1_hi = [ex(f"w1_hi{i}", [P, DC, H], F32R) for i in range(2)]
            w1_lo = [ex(f"w1_lo{i}", [P, DC, H], F32R) for i in range(2)]
            w2_hi = [ex(f"w2_hi{i}", [P, HC, D], F32R) for i in range(2)]
            w2_lo = [ex(f"w2_lo{i}", [P, HC, D], F32R) for i in range(2)]
            b1_all = [ex(f"b1_all{i}", [P, H]) for i in range(2)]
            rowT_h, rowT_l = ex("rowT_h", [P, DC, P], F32R), ex("rowT_l", [P, DC, P], F32R)
            hid = ex("hid", [P, H])
            hidT_h, hidT_l = ex("hidT_h", [P, HC, P], F32R), ex("hidT_l", [P, HC, P], F32R)
            y_sb, y_t, g_sb = ex("y_sb", [P, D]), ex("y_t", [P, D]), ex("g_sb", [P, D])

        u_hi, u_lo = sb("u_hi", [P, DC, S], F32R), sb("u_lo", [P, DC, S], F32R)
        v_hi, v_lo = sb("v_hi", [P, TPB, VW], F32R), sb("v_lo", [P, TPB, VW], F32R)
        theta = sb("theta", [P, 2, S])
        tanh_s = sb("tanh_s", [P, S])
        relu_s = sb("relu_s", [P, S])
        neg_max = sb("neg_max", [P, 2, 2])
        pT_hi = [sb(f"pT_hi{i}", [P, TPB, P], F32R) for i in range(2)]
        pT_lo = [sb(f"pT_lo{i}", [P, TPB, P], F32R) for i in range(2)]
        c_cur = sb("c_cur", [P, 2, TPB])
        rden = sb("rden", [P, 2])
        half_s = sb("half_s", [P, 2, D])
        g_tile = sb("g_tile", [P, 2, D])
        x_tile = sb("x_tile", [P, 2, D])
        slot_cur = sb("slot_cur", [P, 2], I32)

        block = ctx.enter_context(nc.Block())

        chunked = lambda w: w.rearrange("(c p) n -> p c n", p=P)
        S_BANK, PT_BANK, O_BANK = 0, 4, 6
        HID_BANK, HT_BANK, ROW_BANK, Y_BANK = 0, 2, 4, 5

        JT, JU, JV = 4, 4, TPB // 2
        JOBS = JT + JU + JV
        JV0, JV1 = range(JT + JU, JT + JU + JV // 2), range(JT + JU + JV // 2, JOBS)
        def prep_ps(q):
            if q < JT + JU:
                return ps[:, S_BANK + q % 4, :]
            return ps[:, PT_BANK + q - (JT + JU), :]

        KA = K_SIGMOID / 2
        KT, KR = K_TANH / KA, K_RELU / KA

        def wait_apart(engine, semaphore, value):
            engine.wait_ge(semaphore, value)
            engine.sem_inc(passed, 1)

        def zero_padding(engine, parity):
            engine.wait_ge(zeros_ready, 1)
            engine.wait_ge(zero_rows_ready, 1)
            for e in range(parity, E, 2):
                start = engine.value_load(zero_row[0:1, e:e + 1], min_val=0, max_val=E * REGION - P)
                engine.dma_start(sorted_x[bass.ds(start, P), :], zeros[:, :]).then_inc(filled, 16)

        @block.sync
        def _(sp):
            for first, src in ((BQ, bq), (BK, bk), (BV, bv)):
                sp.dma_start(bias_rows[first:first + DC, :], src.rearrange("(c p) -> c p", p=P)).then_inc(small_in, 16)
            for dst, src in ((wo_raw, Wo), (wk_raw, Wk), (wq_raw, Wq), (wv_raw, Wv)):
                sp.dma_start(dst[:, :, 0:D], chunked(src)).then_inc(qkvo_in, 16)
            for b in range(B):
                sp.dma_start(xn_all[:, b * TPB:(b + 1) * TPB, :],
                             x_rows[b * S:(b + 1) * S, :].rearrange("(i p) d -> p i d", p=P)
                             ).then_inc(x_in[b], 16)
            sp.dma_start(b2_all[:, :], b2.rearrange("e (a d) -> a (e d)", a=1).to_broadcast([P, E * D])
                         ).then_inc(b2_in, 16)
            for b in range(B):
                sp.wait_ge(x_in[b], 16)
                sp.sem_inc(x_ready, 1)
            zero_padding(sp, 0)
            sp.wait_ge(tables_ready, 1)
            sp.wait_ge(filled, 16 * E)
            sp.wait_ge(scattered, 16 * NT)

            def load_row(t):
                start = sp.value_load(tile_row[0:1, bass.ds(t, 1)], min_val=0, max_val=E * REGION - P)
                sp.dma_start(row[:, :], sorted_x[bass.ds(start, P), :]).then_inc(row_in, 16)

            load_row(0)
            sp.dma_start(sorted_g[NT * P:, :].rearrange("(i p) d -> p i d", p=P),
                         zeros[:, :].rearrange("p (a d) -> p a d", a=1)
                         .to_broadcast([P, MAX_TILES - NT, D])).then_inc(tail_filled, 16)
            sp.wait_ge(rowT_done, 1)
            load_row(1)
            sp.wait_ge(tail_filled, 16)
            sp.sem_inc(g_stored, 16)
            sp.wait_ge(xn_kept, B)
            sp.wait_ge(lnT_hi, 4 * B)
            sp.dma_start(xn_cur[:, :, :], xn_all[:, 0:TPB, :]).then_inc(cur_in, 16)
            def store_g(t):
                sp.wait_ge(g_ready, t + 1)
                sp.dma_start(sorted_g[bass.ds(t * P, P), :], g_sb[:, :]).then_inc(g_stored, 16)

            sp.wait_ge(rowT_done, 2)
            load_row(AHEAD)
            total = sp.value_load(first_tile[0:1, E:E + 1], min_val=E, max_val=MAX_TILES)
            with sp.Fori(1, total) as t:
                wait_apart(sp, rowT_done, t + AHEAD)
                load_row(t + AHEAD)
                store_g(t - 1)
            store_g(total - 1)
            for j in range(2):
                sp.dma_start(x_tile[:, j, :], x_rows[j * P:(j + 1) * P, :]).then_inc(xt_in[j], 16)

            def batch(b, last):
                if not last:
                    sp.wait_ge(prep_done, b * JOBS + JT)
                    sp.dma_start(xn_cur[:, :, :], xn_all[:, bass.ds(b * TPB + TPB, TPB), :]
                                 ).then_inc(cur_in, 16)
                for j in range(TPB):
                    sp.wait_ge(out_ready, b * TPB + j + 1)
                    sp.dma_start(out_rows[bass.ds(b * S + j * P, P), :], g_tile[:, j % 2, :]
                                 ).then_inc(out_sent[j % 2], 16)
                    if not (last and j + 2 >= TPB):
                        sp.dma_start(x_tile[:, j % 2, :], x_rows[bass.ds(b * S + (j + 2) * P, P), :]
                                     ).then_inc(xt_in[j % 2], 16)

            with sp.Fori(0, B - 1) as b:
                batch(b, False)
            batch(B - 1, True)
            for j in range(2):
                sp.wait_ge(out_sent[j], 16 * NT // 2)

        @block.gpsimd
        def _(pool):
            nc.gpsimd.memset(zeros[:, :], 0.0).then_inc(zeros_ready, 1)
            nc.gpsimd.memset(ident[:, :], 0.0).then_inc(pool_step, 1)
            nc.gpsimd.memset(before[:, :], 1.0).then_inc(pool_step, 1)
            pool.wait_ge(pool_step, 2)
            nc.gpsimd.affine_select(out=ident[:, :], in_=ident[:, :], compare_op=ALU.not_equal, fill=1.0,
                                    base=0, pattern=[[-1, P]], channel_multiplier=1).then_inc(masks_ready, 1)
            nc.gpsimd.affine_select(out=before[:, :], in_=before[:, :], compare_op=ALU.is_gt, fill=0.0,
                                    base=0, pattern=[[1, P]], channel_multiplier=-1).then_inc(masks_ready, 1)
            nc.gpsimd.iota(expert_id[:, :, :], pattern=[[1, E], [0, NT]], base=0, channel_multiplier=0,
                           allow_small_or_imprecise_dtypes=True).then_inc(masks_ready, 1)
            nc.gpsimd.iota(tile_id[:, :], pattern=[[1, TABLE]], base=0, channel_multiplier=0,
                           allow_small_or_imprecise_dtypes=True).then_inc(masks_ready, 1)

            def load_w1(e):
                pool.dma_start(w1_raw[:, :, :], W1[bass.ds(e, 1)].rearrange(
                    "a (c p) n -> p (a c) n", p=P)).then_inc(w1_in, 16)

            def load_w2(e):
                pool.dma_start(w2_raw[:, :, :], W2[bass.ds(e, 1)].rearrange(
                    "a (c p) n -> p (a c) n", p=P)).then_inc(w2_in, 16)

            def load_b1(e, par):
                pool.dma_start(b1_all[par][:, :], b1[bass.ds(e, 1), :].to_broadcast([P, H])).then_inc(b1_in, 16)

            def low_weights(e, hi, lo, raw, high_done, split_done):
                wait_apart(pool, high_done, e + 1)
                nc.gpsimd.tensor_tensor(lo[:, :, :], raw[:, :, :], hi[:, :, :].bitcast(F32), ALU.subtract
                                        ).then_inc(split_done, 1)
                wait_apart(pool, split_done, e + 1)

            def weights(e, par, free, more):
                if free:
                    tiles = pool.value_load(first_tile[0:1, bass.ds(e - 1, 1)], min_val=1, max_val=MAX_TILES)
                    wait_apart(pool, hid_biased, tiles * 2)
                load_b1(e, par)
                low_weights(e, w1_hi[par], w1_lo[par], w1_raw, w1_high, w1_split)
                pool.wait_ge(b1_in, e * 16 + 16)
                pool.sem_inc(b1_ready, 1)
                if more:
                    load_w1(e + 1)
                low_weights(e, w2_hi[par], w2_lo[par], w2_raw, w2_high, w2_split)
                if more:
                    load_w2(e + 1)

            pool.wait_ge(x_ready, 1)
            load_w1(0)
            load_w2(0)
            weights(0, 0, False, True)
            for b in range(B):
                pool.wait_ge(slots_ready, b + 1)
                pool.wait_ge(xn_kept, b + 1)
                for i in range(b * TPB, (b + 1) * TPB):
                    pool.indirect_dma_start(sorted_x, bass.IndirectOffsetOnAxis(ap=slot_i[:, i:i + 1], axis=0),
                                            xn_all[:, i, :], None).then_inc(scattered, 16)
            weights(1, 1, False, True)
            pool.wait_ge(tables_ready, 1)
            with pool.Fori(1, E // 2 - 1) as pair:
                for par in range(2):
                    weights(pair * 2 + par, par, True, True)
            for par in range(2):
                weights(E - 2 + par, par, True, par == 0)
            pool.sem_inc(w1_split, 1)
            pool.sem_inc(b1_ready, 1)

            total = pool.value_load(first_tile[0:1, E:E + 1], min_val=E, max_val=MAX_TILES)
            wait_apart(pool, g_stored, total * 16 + 16)
            pool.wait_ge(slot_g_ready, 1)

            def gather(n, par):
                nc.gpsimd.tensor_copy(slot_cur[:, par:par + 1], slot_g[:, bass.ds(n, 1)]).then_inc(slot_ready, 1)
                wait_apart(pool, slot_ready, n + 1)
                pool.indirect_dma_start(g_tile[:, par, :], None, sorted_g,
                                        bass.IndirectOffsetOnAxis(ap=slot_cur[:, par:par + 1], axis=0)
                                        ).then_inc(g_in[par], 16)

            for n in range(2):
                gather(n, n)
            pool.sem_inc(scaled, 2)

            def batch(b, last):
                for j in range(TPB):
                    n, par = b * TPB + j, j % 2
                    turn = b * (TPB // 2) + j // 2 + 1
                    pool.wait_ge(half_s_ready, n + 1)
                    pool.wait_ge(g_in[par], turn * 16)
                    nc.gpsimd.tensor_tensor(g_tile[:, par, :], half_s[:, par, :], g_tile[:, par, :],
                                            ALU.mult).then_inc(scaled, 1)
                    pool.wait_ge(scaled, n + 3)
                    pool.wait_ge(xt_in[par], turn * 16)
                    nc.gpsimd.tensor_tensor(g_tile[:, par, :], g_tile[:, par, :], x_tile[:, par, :],
                                            ALU.add).then_inc(out_ready, 1)
                    if not (last and j + 2 >= TPB):
                        wait_apart(pool, out_sent[par], turn * 16)
                        gather(n + 2, par)

            with pool.Fori(0, B - 1) as b:
                batch(b, False)
            batch(B - 1, True)

        @block.scalar
        def _(act):
            act.dma_start(bo_row[:, :], bo.rearrange("(a d) -> a d", a=1)).then_inc(router_in, 16)
            act.dma_start(br_all[:, :], br.rearrange("(a e) -> a e", a=1).to_broadcast([P, E])).then_inc(router_in, 16)
            act.dma_start(small_w[:, :, 0:E], chunked(Wr)).then_inc(router_in, 16)
            act.wait_ge(zeros_ready, 1)
            nc.scalar.activation(warm[:, 0:1], zeros[:, 0:1], ACT.Sqrt)
            def square_root(b):
                act.wait_ge(var_ready, b + 1)
                nc.scalar.activation(std[:, :], std[:, :], ACT.Sqrt).then_inc(std_ready, 1)

            square_root(0)
            act.wait_ge(const_pe, 3)
            for m in range(DC):
                nc.scalar.activation(M_hi[:, m, :], ps[:, 2 + m, 0:D], ACT.Copy)
            nc.scalar.activation(G_hi[:, :, :], ps[:, 5, :].rearrange("p (m d) -> p m d", m=DC), ACT.Copy
                                 ).then_inc(const_act, 1)
            def ln_batch(b, more):
                for q in range(4):
                    act.wait_ge(lnT_done, b * 4 + q + 1)
                    nc.scalar.activation(xnT_hi[:, q // 2, (q % 2) * HALF:(q % 2 + 1) * HALF], ps[:, q, :],
                                         ACT.Copy).then_inc(lnT_hi, 1)
                if more:
                    square_root(b + 1)
                nc.scalar.activation(xn_all[:, bass.ds(b * TPB, TPB), :], xn_cur[:, :, :], ACT.Copy
                                     ).then_inc(xn_kept, 1)

            def high_w1(e, par):
                act.wait_ge(w1_in, e * 16 + 16)
                nc.scalar.activation(w1_hi[par][:, :, :], w1_raw[:, :, :], ACT.Copy).then_inc(w1_high, 1)

            def high_w2(e, par):
                act.wait_ge(w2_in, e * 16 + 16)
                nc.scalar.activation(w2_hi[par][:, :, :], w2_raw[:, :, :], ACT.Copy).then_inc(w2_high, 1)

            ln_batch(0, True)
            high_w1(0, 0)
            high_w2(0, 0)
            with act.Fori(1, B - 1) as b:
                ln_batch(b, True)
            ln_batch(B - 1, False)

            def row_high(t):
                act.wait_ge(rowT_done, t + 1)
                nc.scalar.activation(rowT_h[:, :, :], ps[:, ROW_BANK, 0:D].rearrange("p (c n) -> p c n", c=DC),
                                     ACT.Copy).then_inc(rowT_hi, 1)

            def gelus(t):
                for h in range(2):
                    part = hid[:, h * HALF:(h + 1) * HALF]
                    act.wait_ge(hid_biased, t * 2 + h + 1)
                    nc.scalar.activation(part, part, ACT.Gelu).then_inc(gelu_done, 1)

            zero_padding(act, 1)
            high_w1(1, 1)
            high_w2(1, 1)
            nc.scalar.activation(warm[:, 1:2], zeros[:, 0:1], ACT.Gelu)
            act.wait_ge(tables_ready, 1)
            row_high(0)
            gelus(0)
            row_high(1)

            def tile(t, weights=()):
                act.wait_ge(hidT_done, t * 2 + 2)
                nc.scalar.activation(hidT_h[:, HC // 2:, :], ps[:, HT_BANK + 1, :].rearrange(
                    "p (c n) -> p c n", n=P), ACT.Copy).then_inc(hidT_hi1, 1)
                if weights:
                    high_w1(*weights)
                gelus(t + 1)
                row_high(t + AHEAD)
                if weights:
                    high_w2(*weights)
                act.wait_ge(y_biased, t + 1)
                nc.scalar.activation(y_t[:, :], y_sb[:, :], ACT.Tanh, scale=0.5).then_inc(y_tanh, 1)

            def bounds(e):
                return (act.value_load(first_tile[0:1, bass.ds(e, 1)], min_val=0, max_val=MAX_TILES - 1),
                        act.value_load(first_tile[0:1, bass.ds(e + 1, 1)], min_val=1, max_val=MAX_TILES))

            t0, t1 = bounds(0)
            with act.Fori(t0, t1) as t:
                tile(t)
            with act.Fori(0, E // 2 - 1) as pair:
                for par in range(2):
                    e = pair * 2 + par + 1
                    t0, t1 = bounds(e)
                    tile(t0, (e + 1, par))
                    with act.If(t0 + 1 < t1):
                        with act.Fori(t0 + 1, t1) as t:
                            tile(t)
            t0, t1 = bounds(E - 1)
            with act.Fori(t0, t1) as t:
                tile(t)
            nc.scalar.activation(warm[:, 2:3], zeros[:, 0:1], ACT.Exp)

            def high(n_batch, jobs):
                for q in jobs:
                    act.wait_ge(prep_done, n_batch * JOBS + q + 1)
                    if q < JT:
                        nc.scalar.activation(xnT_hi[:, q // 2, (q % 2) * HALF:(q % 2 + 1) * HALF], prep_ps(q),
                                             ACT.Copy).then_inc(prep_hi, 1)
                    elif q < JT + JU:
                        m, h = divmod(q - JT, 2)
                        nc.scalar.activation(u_hi[:, m, h * HALF:(h + 1) * HALF], prep_ps(q), ACT.Identity,
                                             bias=r_col[:, m:m + 1]).then_inc(prep_hi, 1)
                    else:
                        i = 2 * (q - JT - JU)
                        nc.scalar.activation(v_hi[:, i:i + 2, 0:D], prep_ps(q).rearrange("p (i d) -> p i d", d=D),
                                             ACT.Copy).then_inc(prep_hi, 1)

            def tanhs(n, j, h):
                bank, cols = ps[:, S_BANK + 2 * (j % 2) + h, :], slice(h * HALF, (h + 1) * HALF)
                act.wait_ge(scores_done, n * 2 + h + 1)
                nc.scalar.activation(theta[:, j % 2, cols], bank, ACT.Tanh, bias=c_cur[:, 1, j:j + 1], scale=0.5)
                nc.scalar.activation(tanh_s[:, cols], bank, ACT.Tanh, bias=c_cur[:, 0, j:j + 1]
                                     ).then_inc(tanhs_done, 1)

            def relu(j, h):
                nc.scalar.activation(relu_s[:, h * HALF:(h + 1) * HALF], ps[:, S_BANK + 2 * (j % 2) + h, :], ACT.Relu,
                                     bias=c_cur[:, 0, j:j + 1], scale=KR).then_inc(acts_done, 1)

            def exps(n, j):
                act.wait_ge(theta_done, n + 1)
                for h in range(2):
                    part = theta[:, j % 2, h * HALF:(h + 1) * HALF]
                    nc.scalar.activation(part, part, ACT.Exp, bias=neg_max[:, j % 2, 1:2], scale=-1.0
                                         ).then_inc(exp_done, 1)

            assert KR == 1.0

            def acts(n, j):
                for h in range(2):
                    tanhs(n, j, h)
                    relu(j, h)

            def transposed_high(n, j):
                act.wait_ge(pT_done, n * 2 + 2)
                nc.scalar.activation(pT_hi[j % 2][:, TPB // 2:, :], ps[:, PT_BANK + 1, :].rearrange(
                    "p (c n) -> p c n", n=P), ACT.Copy).then_inc(pT_hi1, 1)

            def begin_batch(nb):
                act.wait_ge(c_ready, nb + 1)
                acts(nb * TPB, 0)
                high(nb, JV0)
                exps(nb * TPB, 0)

            def batch(b, last):
                for j in range(TPB):
                    n = b * TPB + j
                    if j + 1 < TPB:
                        acts(n + 1, j + 1)
                        if j == 0:
                            high(b, JV1)
                        transposed_high(n, j)
                        exps(n + 1, j + 1)
                    else:
                        if not last:
                            high(b + 1, range(0, JT))
                        transposed_high(n, j)
                        if not last:
                            high(b + 1, range(JT, JT + JU))
                            begin_batch(b + 1)

            high(0, range(JT + JU))
            begin_batch(0)
            with act.Fori(0, B - 1) as b:
                batch(b, False)
            batch(B - 1, True)

        @block.tensor
        def _(pe):
            mm = nc.tensor.matmul

            def product(dst, a_hi, a_lo, b_hi, b_lo, first, last):
                mm(dst, a_hi, b_hi, start=first, stop=False)
                mm(dst, a_hi, b_lo, start=False, stop=False)
                return mm(dst, a_lo, b_hi, start=False, stop=last)

            pe.wait_ge(masks_ready, 1)
            pe.wait_ge(small_in, 16 * 3)
            nr = 3 * DC
            nc.tensor.transpose(ps[:, 0, 0:nr], bias_rows[:, :], ident[0:nr, 0:nr]).then_inc(const_pe, 1)
            pe.wait_ge(qkvo_in, 16 * 4)
            for ec in range(DC):
                for fc in range(DC):
                    last = nc.tensor.transpose(ps[:, 1, ec * D + fc * P:ec * D + (fc + 1) * P],
                                               wo_raw[:, fc, ec * P:(ec + 1) * P], ident[:, :])
            last.then_inc(const_pe, 1)
            pe.wait_ge(const_dve, 1)
            for m in range(DC):
                for ec in range(DC):
                    mm(ps[:, 2 + m, 0:D + 1], wq_raw[:, ec, m * P:(m + 1) * P], wk_raw[:, ec, :],
                       start=ec == 0, stop=ec == DC - 1)
            for m in range(DC):
                for ec in range(DC):
                    mm(ps[:, 4, m:m + 1], wk_raw[:, ec, m * P:(m + 1) * P], bias_cols[:, BQ + ec:BQ + ec + 1],
                       start=ec == 0, stop=ec == DC - 1)
            for ec in range(DC):
                mm(ps[:, 4, DC:DC + 1], bq_wide[:, ec, :], bias_cols[:, BK + ec:BK + ec + 1],
                   start=ec == 0, stop=ec == DC - 1)
            for m in range(DC):
                for ec in range(DC):
                    mm(ps[:, 5, m * D:(m + 1) * D], wv_raw[:, ec, m * P:(m + 1) * P], woT[:, ec, :],
                       start=ec == 0, stop=ec == DC - 1)
            pe.wait_ge(router_in, 16 * 3)
            for ec in range(DC):
                mm(ps[:, 6, 0:D], bv_wide[:, ec, :], woT[:, ec, :], start=ec == 0, stop=False)
            mm(ps[:, 6, 0:D], ones[0:1, :], bo_row[:, :], start=False, stop=True).then_inc(const_pe, 1)

            pe.wait_ge(const_dve, 2)
            def turn_batch(b):
                pe.wait_ge(xn_ready, b + 1)
                for q in range(4):
                    k, i0 = q // 2, (q % 2) * 4
                    for i in range(4):
                        last = nc.tensor.transpose(ps[:, q, i * P:(i + 1) * P],
                                                   xn_cur[:, i0 + i, k * P:(k + 1) * P], ident[:, :])
                    last.then_inc(lnT_done, 1)

            def route(b, more):
                pe.wait_ge(lnT_lo, b * 4 + 4)
                for i in range(TPB):
                    cols, dst = slice(i * P, (i + 1) * P), ps[:, 4, i * 2 * SM:(i + 1) * 2 * SM]
                    mm(dst, xnT_hi[:, 0, cols], R_parts[:, 0, :, :], start=True, stop=False)
                    for k in range(DC):
                        mm(dst[:, 0:SM], xnT_lo[:, k, cols], R_parts[:, k, 0, :], start=False, stop=False)
                    last = mm(dst, xnT_hi[:, 1, cols], R_parts[:, 1, :, :], start=False, stop=True)
                last.then_inc(logits_done, 1)
                if more:
                    turn_batch(b + 1)
                ranks = ps[:, 5, 0:E * TPB]
                pe.wait_ge(onehot_ready, b + 1)
                mm(ranks, before[:, :], onehot[:, :, 1:], start=True, stop=False)
                mm(ranks, ones[:, :], running[:, :, 0:TPB], start=False, stop=True).then_inc(ranks_done, 1)

            turn_batch(0)
            with pe.Fori(0, B - 1) as b:
                route(b, True)
            route(B - 1, False)
            pe.wait_ge(carry_ready, 1)
            mm(ps[:, 6, 0:E], ones[:, :], onehot[:, :, 0], start=True, stop=True).then_inc(counts_done, 1)

            def turn_row(t):
                pe.wait_ge(row_in, t * 16 + 16)
                for k in range(DC):
                    last = nc.tensor.transpose(ps[:, ROW_BANK, k * P:(k + 1) * P], row[:, k * P:(k + 1) * P],
                                               ident[:, :])
                last.then_inc(rowT_done, 1)

            def hidden(t, par):
                pe.wait_ge(rowT_ready, t + 1)
                for h in range(2):
                    for k in range(DC):
                        cols = slice(h * HALF, (h + 1) * HALF)
                        last = product(ps[:, HID_BANK + h, :], rowT_h[:, k, :], rowT_l[:, k, :],
                                       w1_hi[par][:, k, cols], w1_lo[par][:, k, cols], k == 0, k == DC - 1)
                    last.then_inc(hid_done, 1)

            def tile(t, par, next_par, ends=None):
                for h in range(2):
                    pe.wait_ge(gelu_done, t * 2 + h + 1)
                    for i in range(h * 4, h * 4 + 4):
                        last = nc.tensor.transpose(ps[:, HT_BANK + h, (i % 4) * P:(i % 4 + 1) * P],
                                                   hid[:, i * P:(i + 1) * P], ident[:, :])
                    last.then_inc(hidT_done, 1)
                if ends is not None:
                    wait_apart(pe, w1_split, ends + 2)
                hidden(t + 1, next_par)
                turn_row(t + AHEAD)
                for i in range(HC):
                    if i % 4 == 0:
                        pe.wait_ge(hidT_ready, t * 2 + i // 4 + 1)
                    last = product(ps[:, Y_BANK, 0:D], hidT_h[:, i, :], hidT_l[:, i, :],
                                   w2_hi[par][:, i, :], w2_lo[par][:, i, :], i == 0, i == HC - 1)
                last.then_inc(y_done, 1)

            pe.wait_ge(tables_ready, 1)
            turn_row(0)
            pe.wait_ge(w1_split, 1)
            hidden(0, 0)
            turn_row(1)
            with pe.Fori(0, E // 2) as pair:
                for par in range(2):
                    e = pair * 2 + par
                    wait_apart(pe, w2_split, e + 1)
                    t0 = pe.value_load(first_tile[0:1, bass.ds(e, 1)], min_val=0, max_val=MAX_TILES - 1)
                    t1 = pe.value_load(last_tile[0:1, bass.ds(e, 1)], min_val=0, max_val=MAX_TILES - 1)
                    with pe.If(t0 < t1):
                        with pe.Fori(t0, t1) as t:
                            tile(t, par, par)
                    tile(t1, par, 1 - par, e)

            total = pe.value_load(first_tile[0:1, E:E + 1], min_val=E, max_val=MAX_TILES)
            wait_apart(pe, rowT_ready, total + AHEAD)

            def prepare(nb, jobs):
                for q in jobs:
                    bank = prep_ps(q)
                    if q < JT:
                        if q == 0:
                            pe.wait_ge(cur_in, nb * 16 + 16)
                        k, i0 = q // 2, (q % 2) * 4
                        for i in range(4):
                            last = nc.tensor.transpose(bank[:, i * P:(i + 1) * P],
                                                       xn_cur[:, i0 + i, k * P:(k + 1) * P], ident[:, :])
                    elif q < JT + JU:
                        if q == JT:
                            pe.wait_ge(prep_ready, nb * JOBS + JT)
                        m, h = divmod(q - JT, 2)
                        for k in range(DC):
                            rows, cols = slice(m * P, (m + 1) * P), slice(h * HALF, (h + 1) * HALF)
                            last = product(bank, M_hi[:, k, rows], M_lo[:, k, rows],
                                           xnT_hi[:, k, cols], xnT_lo[:, k, cols], k == 0, k == DC - 1)
                    else:
                        for i in range(2):
                            tile = 2 * (q - JT - JU) + i
                            cols = slice(tile * P, (tile + 1) * P)
                            for k in range(DC):
                                last = product(bank[:, i * D:(i + 1) * D], xnT_hi[:, k, cols], xnT_lo[:, k, cols],
                                               G_hi[:, k, :], G_lo[:, k, :], k == 0, k == DC - 1)
                    last.then_inc(prep_done, 1)

            def scores(n, j):
                for h in range(2):
                    for k in range(DC):
                        rows, cols = slice(j * P, (j + 1) * P), slice(h * HALF, (h + 1) * HALF)
                        last = product(ps[:, S_BANK + 2 * (j % 2) + h, :], u_hi[:, k, rows], u_lo[:, k, rows],
                                       xnT_hi[:, k, cols], xnT_lo[:, k, cols], k == 0, k == DC - 1)
                    last.then_inc(scores_done, 1)

            def transposes(n, j):
                for h in range(2):
                    pe.wait_ge(exp_done, n * 2 + h + 1)
                    for i in range(4):
                        last = nc.tensor.transpose(
                            ps[:, PT_BANK + h, i * P:(i + 1) * P],
                            theta[:, j % 2, h * HALF + i * P:h * HALF + (i + 1) * P], ident[:, :])
                    last.then_inc(pT_done, 1)

            def values(n, j):
                for i in range(TPB):
                    if i % 4 == 0:
                        pe.wait_ge(pT_ready, n * 2 + i // 4 + 1)
                    last = product(ps[:, O_BANK + j % 2, 0:VW], pT_hi[j % 2][:, i, :], pT_lo[j % 2][:, i, :],
                                   v_hi[:, i, :], v_lo[:, i, :], i == 0, i == TPB - 1)
                last.then_inc(pv_done, 1)

            def first_scores(nb):
                pe.wait_ge(prep_ready, nb * JOBS + JT + JU)
                scores(nb * TPB, 0)
                prepare(nb, JV0)

            def batch(b, last_batch):
                for j in range(TPB):
                    n = b * TPB + j
                    if j + 1 < TPB:
                        scores(n + 1, j + 1)
                        if j == 0:
                            pe.wait_ge(prep_ready, b * JOBS + JT + JU + len(JV0))
                            prepare(b, JV1)
                    elif not last_batch:
                        pe.wait_ge(acts_done, n * 2 + 2)
                        prepare(b + 1, range(0, JT))
                    if j + 1 == TPB:
                        values(n - 1, j - 1)
                    elif j > 0:
                        pe.wait_ge(pT_ready, n * 2)
                    transposes(n, j)
                    if j == 1:
                        pe.wait_ge(prep_ready, b * JOBS + JOBS)
                    if 0 < j < TPB - 1:
                        values(n - 1, j - 1)
                if not last_batch:
                    prepare(b + 1, range(JT, JT + JU))
                values(n, TPB - 1)
                if not last_batch:
                    first_scores(b + 1)

            prepare(0, range(JT + JU))
            first_scores(0)
            with pe.Fori(0, B - 1) as b:
                batch(b, False)
            batch(B - 1, True)

        @block.vector
        def _(dve):
            v = nc.vector
            steps = [0]

            def step(ins):
                steps[0] += 1
                ins.then_inc(dve_step, 1)
                dve.wait_ge(dve_step, steps[0])

            v.memset(ones[:, :], 1.0)
            v.memset(keep_scan[:, :, :], 1.0)
            step(v.memset(small_w[:, :, E + 1:SM], 0.0))
            v.memset(onehot[:, :, 0:1], 0.0)
            step(v.memset(keep_scan[:, :, 0:1], 0.0))
            dve.wait_ge(const_pe, 1)
            step(v.tensor_copy(bias_cols[:, :], ps[:, 0, 0:3 * DC]))
            dve.wait_ge(qkvo_in, 16 * 4)
            for ec in range(DC):
                v.tensor_copy(wk_raw[:, ec, D:D + 1], bias_cols[:, BK + ec:BK + ec + 1])
                v.tensor_scalar(bq_wide[:, ec, :], ones[:, :], bias_cols[:, BQ + ec:BQ + ec + 1], None, ALU.mult)
                v.tensor_scalar(bv_wide[:, ec, :], ones[:, :], bias_cols[:, BV + ec:BV + ec + 1], None, ALU.mult)
            dve.wait_ge(const_pe, 2)
            v.tensor_copy(woT[:, :, :], ps[:, 1, :].rearrange("p (c f) -> p c f", c=DC)).then_inc(const_dve, 1)
            LN_STEPS, SORT_STEPS = 3, 11

            def statistics(b):
                dve.wait_ge(x_ready, b + 1)
                for i in range(TPB):
                    last = v.bn_stats(stats[:, i, :], xn_all[:, bass.ds(b * TPB + i, 1), :])
                last.then_inc(ln_step, 1)
                wait_apart(dve, ln_step, b * LN_STEPS + 1)
                for i in range(TPB):
                    last = v.bn_aggr(mean_var[:, i, :], stats[:, i, :])
                last.then_inc(ln_step, 1)
                dve.wait_ge(ln_step, b * LN_STEPS + 2)
                v.tensor_scalar(std[:, :], mean_var[:, :, 1], LN_EPS, None, ALU.add).then_inc(var_ready, 1)

            def normalize(b):
                dve.wait_ge(std_ready, b + 1)
                v.reciprocal(rstd[:, :], std[:, :]).then_inc(ln_step, 1)
                wait_apart(dve, ln_step, b * LN_STEPS + 3)
                for i in range(TPB):
                    last = v.tensor_scalar(xn_cur[:, i, :], xn_all[:, bass.ds(b * TPB + i, 1), :],
                                           mean_var[:, i, 0:1], rstd[:, i:i + 1], ALU.subtract, ALU.mult)
                last.then_inc(xn_ready, 1)

            statistics(0)
            normalize(0)
            dve.wait_ge(const_pe, 3)
            dve.wait_ge(const_act, 1)
            dve.wait_ge(router_in, 16 * 3)
            for m in range(DC):
                v.tensor_copy(small_w[:, m, E:E + 1], ps[:, 2 + m, D:D + 1])
            v.tensor_copy(r_col[:, :], ps[:, 4, 0:DC])
            v.tensor_copy(kappa[:, :], ps[:, 4, DC:DC + 1])
            step(v.tensor_scalar(attn_const[:, :], ps[:, 6, 0:D], 0.5, None, ALU.mult))
            step(v.tensor_copy(R_parts[:, :, 0, :], small_w[:, :, :]))
            v.tensor_tensor(R_parts[:, :, 1, :], small_w[:, :, :], R_parts[:, :, 0, :].bitcast(F32), ALU.subtract)
            for m in range(DC):
                v.tensor_tensor(M_lo[:, m, :], ps[:, 2 + m, 0:D], M_hi[:, m, :].bitcast(F32), ALU.subtract)
            v.tensor_tensor(G_lo[:, :, :], ps[:, 5, :].rearrange("p (m d) -> p m d", m=DC),
                            G_hi[:, :, :].bitcast(F32), ALU.subtract).then_inc(const_dve, 1)

            by_token = lambda a: a.rearrange("p e i -> p i e")
            over_experts = lambda a, n: a.rearrange("p (a i) -> p a i", a=1).to_broadcast([P, E, n])
            over_tiles = lambda a, n: a.rearrange("p (e a) -> p e a", a=1).to_broadcast([P, E, n])
            flat = lambda a: a[:, :, :].rearrange("p e i -> p (e i)")

            def route(b):
                count = [0]
                now = bass.ds(b * TPB, TPB)

                def then(ins):
                    count[0] += 1
                    ins.then_inc(sort_step, 1)
                    wait_apart(dve, sort_step, b * SORT_STEPS + count[0])

                dve.wait_ge(logits_done, b + 1)
                small = ps[:, 4, 0:TPB * 2 * SM].rearrange("p (i h s) -> p i h s", h=2, s=SM)
                v.tensor_scalar(c_all[:, now], small[:, :, 0, E], kappa[:, 0:1], None, ALU.add)
                then(v.tensor_tensor(by_token(logits[:, 0]), small[:, :, 0, 0:E],
                                     br_all[:, :].rearrange("p (a e) -> p a e", a=1).to_broadcast([P, TPB, E]),
                                     ALU.add))
                v.tensor_tensor(c_all[:, now], c_all[:, now], small[:, :, 1, E], ALU.add)
                then(v.tensor_tensor(by_token(logits[:, 1]), by_token(logits[:, 0]), small[:, :, 1, 0:E], ALU.add))
                then(v.tensor_reduce(best[:, :], by_token(logits[:, 1]), X, ALU.max))
                then(v.tensor_tensor(logits[:, 0], logits[:, 1], over_experts(best[:, :], TPB), ALU.is_ge))
                then(v.scalar_tensor_tensor(tagged[:, :, :], logits[:, 0], float(-E), expert_id[:, :, 0:TPB],
                                            ALU.mult, ALU.add))
                then(v.tensor_reduce(tag_all[:, now], by_token(tagged[:, :, :]), X, ALU.min))
                then(v.tensor_tensor(onehot[:, :, 1:], tagged[:, :, :], over_experts(tag_all[:, now], TPB),
                                     ALU.is_equal))
                v.tensor_tensor_scan(flat(running), flat(keep_scan), flat(onehot), 0.0, ALU.mult, ALU.add
                                     ).then_inc(onehot_ready, 1)
                dve.wait_ge(ranks_done, b + 1)
                then(v.tensor_copy(onehot[:, :, 0], running[:, :, TPB]))
                then(v.tensor_tensor(rank[:, :, :], ps[:, 5, 0:E * TPB].rearrange("p (e i) -> p e i", e=E),
                                     onehot[:, :, 1:], ALU.mult))
                then(v.tensor_reduce(rank_all[:, now], by_token(rank[:, :, :]), X, ALU.add))
                then(v.scalar_tensor_tensor(slot_f[:, :], tag_all[:, now], float(REGION), rank_all[:, now],
                                            ALU.mult, ALU.add))
                v.tensor_scalar(slot_i[:, now], slot_f[:, :], float(E * REGION), None, ALU.add
                                ).then_inc(slots_ready, 1)
                assert count[0] == SORT_STEPS

            def low_ln(b):
                for q in range(4):
                    cols = slice((q % 2) * HALF, (q % 2 + 1) * HALF)
                    dve.wait_ge(lnT_hi, b * 4 + q + 1)
                    v.tensor_tensor(xnT_lo[:, q // 2, cols], ps[:, q, :], xnT_hi[:, q // 2, cols].bitcast(F32),
                                    ALU.subtract).then_inc(lnT_lo, 1)

            dve.wait_ge(masks_ready, 4)

            def ln_batch(b, left):
                low_ln(b)
                if left > 1:
                    dve.wait_ge(xn_kept, b + 1)
                    normalize(b + 1)
                if left > 2:
                    statistics(b + 2)
                route(b)

            statistics(1)
            with dve.Fori(0, B - 2) as b:
                ln_batch(b, 3)
            ln_batch(B - 2, 2)
            ln_batch(B - 1, 1)

            dve.sem_inc(carry_ready, 1)
            dve.wait_ge(counts_done, 1)
            counts = ps[:, 6, 0:E]
            v.scalar_tensor_tensor(zero_row[:, :], expert_id[:, :, 0], float(REGION), counts, ALU.mult, ALU.add
                                   ).then_inc(zero_rows_ready, 1)
            step(v.tensor_scalar(tiles_i[:, 0, :], counts, float(P - 1), None, ALU.add))
            step(v.tensor_scalar(tiles_i[:, 1, :], tiles_i[:, 0, :], 7, None, ALU.arith_shift_right))
            step(v.tensor_scalar(tiles_f[:, 0, :], tiles_i[:, 1, :], 1.0, None, ALU.max))
            step(v.tensor_tensor_scan(tiles_f[:, 1, :], ones[:, 0:E], tiles_f[:, 0, :], 0.0, ALU.mult, ALU.add))
            v.memset(first_tile[:, 0:1], 0)
            v.memset(gap[:, 0:1], 0.0)
            v.tensor_copy(first_tile[:, 1:E + 1], tiles_f[:, 1, :])
            v.tensor_scalar(last_tile[:, :], tiles_f[:, 1, :], -1.0, None, ALU.add)
            v.tensor_scalar(last_used[:, :], tiles_f[:, 1, E - 1:E], -1.0, None, ALU.add)
            v.tensor_scalar(gap[:, 1:E], tiles_f[:, 0, 0:E - 1], float(-P), float(REGION), ALU.mult, ALU.add)
            step(v.tensor_tensor(tiles_f[:, 2, :], tiles_f[:, 1, :], tiles_f[:, 0, :], ALU.subtract))
            step(v.tensor_scalar(used_tile[:, :], tile_id[:, :], last_used[:, 0:1], None, ALU.min))
            step(v.tensor_tensor(after[:, :, :], over_experts(used_tile[:, :], TABLE),
                                 over_tiles(tiles_f[:, 2, :], TABLE), ALU.is_ge))
            step(v.tensor_tensor(after[:, :, :], after[:, :, :], over_tiles(gap[:, :], TABLE), ALU.mult))
            step(v.tensor_reduce(skipped[:, :], by_token(after[:, :, :]), X, ALU.add))
            v.scalar_tensor_tensor(tile_row[:, :], used_tile[:, :], float(P), skipped[:, :], ALU.mult, ALU.add
                                   ).then_inc(tables_ready, 1)
            step(v.tensor_scalar(tag_all[:, :], tag_all[:, :], float(E), None, ALU.add))
            step(v.tensor_tensor(chosen[:, :, :], over_experts(tag_all[:, :], NT), expert_id[:, :, :], ALU.is_equal))
            step(v.tensor_tensor(chosen[:, :, :], chosen[:, :, :], over_tiles(tiles_f[:, 2, :], NT), ALU.mult))
            step(v.tensor_reduce(first_slot[:, :], by_token(chosen[:, :, :]), X, ALU.add))
            v.scalar_tensor_tensor(slot_g[:, :], first_slot[:, :], float(P), rank_all[:, :], ALU.mult, ALU.add
                                   ).then_inc(slot_g_ready, 1)

            def row_low(t):
                dve.wait_ge(rowT_hi, t + 1)
                v.tensor_tensor(rowT_l[:, :, :], ps[:, ROW_BANK, 0:D].rearrange("p (c n) -> p c n", c=DC),
                                rowT_h[:, :, :].bitcast(F32), ALU.subtract).then_inc(rowT_ready, 1)

            def add_b1(t, par):
                for h in range(2):
                    cols = slice(h * HALF, (h + 1) * HALF)
                    dve.wait_ge(hid_done, t * 2 + h + 1)
                    v.tensor_tensor(hid[:, cols], ps[:, HID_BANK + h, :], b1_all[par][:, cols], ALU.add
                                    ).then_inc(hid_biased, 1)

            def tile(t, e, next_par, ends=False):
                hid_bank = [ps[:, HT_BANK + h, :].rearrange("p (c n) -> p c n", n=P) for h in range(2)]
                dve.wait_ge(hidT_done, t * 2 + 1)
                v.tensor_copy(hidT_h[:, 0:4, :], hid_bank[0]).then_inc(hidT_hi0, 1)
                dve.wait_ge(hidT_hi0, t + 1)
                v.tensor_tensor(hidT_l[:, 0:4, :], hid_bank[0], hidT_h[:, 0:4, :].bitcast(F32), ALU.subtract
                                ).then_inc(hidT_ready, 1)
                dve.wait_ge(hidT_hi1, t + 1)
                v.tensor_tensor(hidT_l[:, 4:8, :], hid_bank[1], hidT_h[:, 4:8, :].bitcast(F32), ALU.subtract
                                ).then_inc(hidT_ready, 1)
                if ends:
                    wait_apart(dve, b1_ready, e + 2)
                add_b1(t + 1, next_par)
                row_low(t + AHEAD)
                dve.wait_ge(y_done, t + 1)
                v.tensor_tensor(y_sb[:, :], ps[:, Y_BANK, 0:D], b2_all[:, bass.ds(e * D, D)], ALU.add
                                ).then_inc(y_biased, 1)
                dve.wait_ge(y_tanh, t + 1)
                dve.wait_ge(g_stored, t * 16 + 16)
                v.scalar_tensor_tensor(g_sb[:, :], y_t[:, :], 1.0, y_sb[:, :], ALU.add, ALU.mult
                                       ).then_inc(g_ready, 1)

            dve.wait_ge(slot_g_ready, 1)
            dve.wait_ge(b2_in, 16)
            dve.wait_ge(b1_ready, 1)
            row_low(0)
            add_b1(0, 0)
            row_low(1)
            with dve.Fori(0, E // 2) as pair:
                for par in range(2):
                    e = pair * 2 + par
                    t0 = dve.value_load(first_tile[0:1, bass.ds(e, 1)], min_val=0, max_val=MAX_TILES - 1)
                    t1 = dve.value_load(last_tile[0:1, bass.ds(e, 1)], min_val=0, max_val=MAX_TILES - 1)
                    with dve.If(t0 < t1):
                        with dve.Fori(t0, t1) as t:
                            tile(t, e, par)
                    tile(t1, e, 1 - par, True)

            def low(nb, jobs):
                for q in jobs:
                    dve.wait_ge(prep_hi, nb * JOBS + q + 1)
                    if q < JT:
                        cols = slice((q % 2) * HALF, (q % 2 + 1) * HALF)
                        v.tensor_tensor(xnT_lo[:, q // 2, cols], prep_ps(q), xnT_hi[:, q // 2, cols].bitcast(F32),
                                        ALU.subtract).then_inc(prep_ready, 1)
                    elif q < JT + JU:
                        m, h = divmod(q - JT, 2)
                        cols = slice(h * HALF, (h + 1) * HALF)
                        v.scalar_tensor_tensor(u_lo[:, m, cols], prep_ps(q), r_col[:, m:m + 1],
                                               u_hi[:, m, cols].bitcast(F32), ALU.add, ALU.subtract
                                               ).then_inc(prep_ready, 1)
                    else:
                        i = 2 * (q - JT - JU)
                        v.tensor_tensor(v_lo[:, i:i + 2, 0:D], prep_ps(q).rearrange("p (i d) -> p i d", d=D),
                                        v_hi[:, i:i + 2, 0:D].bitcast(F32), ALU.subtract).then_inc(prep_ready, 1)

            def batch_c(nb):
                v.tensor_copy(c_cur[:, 0, :], c_all[:, bass.ds(nb * TPB, TPB)])
                v.tensor_scalar(c_cur[:, 1, :], c_all[:, bass.ds(nb * TPB, TPB)], 0.5, None, ALU.mult
                                ).then_inc(c_ready, 1)

            def thetas(n, j):
                for h in range(2):
                    cols = slice(h * HALF, (h + 1) * HALF)
                    part = theta[:, j % 2, cols]
                    dve.wait_ge(tanhs_done, n * 2 + h + 1)
                    v.scalar_tensor_tensor(part, tanh_s[:, cols], KT, part, ALU.mult, ALU.add).then_inc(mixed, 1)
                    wait_apart(dve, mixed, n * 3 + 2 * h + 1)
                    wait_apart(dve, acts_done, n * 2 + h + 1)
                    least = neg_max[:, j % 2, h:h + 1]
                    ins = v.tensor_tensor_reduce(out=part, in0=part, in1=relu_s[:, cols], scale=-KA,
                                                 scalar=3.0e38 if h == 0 else neg_max[:, j % 2, 0:1],
                                                 op0=ALU.add, op1=ALU.min, accum_out=least)
                    ins.then_inc(mixed if h == 0 else theta_done, 1)
                    if h == 0:
                        wait_apart(dve, mixed, n * 3 + 2)

            def finish(n, j):
                dve.wait_ge(pv_done, n + 1)
                v.reciprocal(rden[:, j % 2:j % 2 + 1], ps[:, O_BANK + j % 2, D:D + 1]).then_inc(rden_ready, 1)
                dve.wait_ge(rden_ready, n + 1)
                dve.wait_ge(scaled, n + 1)
                v.scalar_tensor_tensor(half_s[:, j % 2, :], ps[:, O_BANK + j % 2, 0:D], rden[:, j % 2:j % 2 + 1], attn_const[:, :],
                                       ALU.mult, ALU.add).then_inc(half_s_ready, 1)

            def transposed_parts(n, j):
                dve.wait_ge(pT_done, n * 2 + 1)
                bank = [ps[:, PT_BANK + h, :].rearrange("p (c n) -> p c n", n=P) for h in range(2)]
                hi, lo = pT_hi[j % 2], pT_lo[j % 2]
                v.tensor_copy(hi[:, 0:4, :], bank[0]).then_inc(pT_hi0, 1)
                dve.wait_ge(pT_hi0, n + 1)
                v.tensor_tensor(lo[:, 0:4, :], bank[0], hi[:, 0:4, :].bitcast(F32), ALU.subtract).then_inc(pT_ready, 1)
                dve.wait_ge(pT_hi1, n + 1)
                v.tensor_tensor(lo[:, 4:8, :], bank[1], hi[:, 4:8, :].bitcast(F32), ALU.subtract).then_inc(pT_ready, 1)

            def batch(b, last):
                for j in range(TPB):
                    n = b * TPB + j
                    if j + 1 < TPB:
                        thetas(n + 1, j + 1)
                        if j == 0:
                            low(b, JV1)
                    elif not last:
                        low(b + 1, range(0, JT))
                    transposed_parts(n, j)
                    if j:
                        finish(n - 1, j - 1)
                if not last:
                    low(b + 1, range(JT, JT + JU))
                    batch_c(b + 1)
                finish(n, TPB - 1)
                if not last:
                    thetas(n + 1, 0)
                    low(b + 1, JV0)

            v.memset(v_hi[:, :, D:D + 1].bitcast(F32), 2.0)
            v.memset(v_hi[:, :, D + 1:VW].bitcast(F32), 0.0)
            v.memset(v_lo[:, :, D:VW].bitcast(F32), 0.0)
            batch_c(0)
            low(0, range(JT + JU))
            thetas(0, 0)
            low(0, JV0)
            with dve.Fori(0, B - 1) as b:
                batch(b, False)
            batch(B - 1, True)


_INS = ['L0_attn_x', 'L0_attn_Wq', 'L0_attn_bq', 'L0_attn_Wk', 'L0_attn_bk', 'L0_attn_Wv', 'L0_attn_bv', 'L0_attn_Wo',
        'L0_attn_bo', 'L0_ffn_Wr', 'L0_ffn_br', 'L0_ffn_W1', 'L0_ffn_b1', 'L0_ffn_W2', 'L0_ffn_b2']


def kernel(**inputs):
    import numpy as _np
    import concourse.bacc as _bacc
    from concourse import mybir as _mybir
    from concourse.bass_utils import run_bass_kernel_spmd as _run

    nc = _bacc.Bacc("TRN2", target_bir_lowering=False, num_devices=1)
    arrays, args = {}, []
    for name in _INS:
        a = _np.ascontiguousarray(inputs[name])
        arrays[f"in_{name}_dram"] = a
        args.append(nc.dram_tensor(f"in_{name}_dram", a.shape, _mybir.dt.from_np(a.dtype), kind="ExternalInput").ap())
    shape = tuple(inputs['L0_attn_x'].shape)
    args.append(nc.dram_tensor("out_0_dram", shape, F32, kind="ExternalOutput").ap())
    block_attention_moe(nc, *args)
    r = _run(nc, [arrays], core_ids=[0])
    return r.results[0]["out_0_dram"]
```

```python
from contextlib import ExitStack

import concourse.bass as bass
from concourse import mybir

P = 128
F32 = mybir.dt.float32
F32R = mybir.dt.float32r
I32 = mybir.dt.int32
ALU = mybir.AluOpType
ACT = mybir.ActivationFunctionType
X = mybir.AxisListType.X

LN_EPS = 1e-5
BASE_THETA, K_SIGMOID, K_TANH, K_RELU = 0.5, 0.2, 0.15, 0.1


def block_attention_moe(nc, x, Wq, bq, Wk, bk, Wv, bv, Wo, bo, Wr, br, W1, b1, W2, b2, out):
    B, S, D = x.shape
    E, _, H = W1.shape
    DC = D // P
    HC = H // P
    TPB = S // P
    NT = B * TPB
    MAX_TILES = NT + E - 1
    HALF = S // 2
    AHEAD = 2
    TABLE = MAX_TILES + AHEAD
    SM = E + 2
    VW = D + 2
    assert (P, DC, HALF) == (128, 2, 512) and TPB == 8

    x_rows = x.rearrange("b s d -> (b s) d")
    out_rows = out.rearrange("b s d -> (b s) d")
    REGION = (NT + 1) * P
    sorted_x = nc.dram_tensor("sorted_x", (E * REGION, D), F32, kind="Internal").ap()
    sorted_g = nc.dram_tensor("sorted_g", (MAX_TILES * P, D), F32, kind="Internal").ap()

    with ExitStack() as ctx:
        def sb(name, shape, dt=F32):
            return ctx.enter_context(nc.sbuf_tensor(name, shape, dt))

        def sem(name):
            return ctx.enter_context(nc.semaphore(name))

        ps = ctx.enter_context(nc.psum_tensor("ps", [P, 8, 512], F32))

        ident = sb("ident", [P, P])
        before = sb("before", [P, P])
        before_r, ones_r = sb("before_r", [P, P], F32R), sb("ones_r", [P, P], F32R)
        ones = sb("ones", [P, P])
        zeros = sb("zeros", [P, D])
        warm = sb("warm", [P, 3])
        bias_rows = sb("bias_rows", [3 * DC, P])
        bias_cols = sb("bias_cols", [P, 3 * DC])
        BQ, BK, BV = 0, DC, 2 * DC
        bo_row = sb("bo_row", [1, D])
        br_all = sb("br_all", [P, E])
        b2_all = sb("b2_all", [P, E * D])
        kappa = sb("kappa", [P, 1])
        r_col = sb("r_col", [P, DC])
        attn_const = sb("attn_const", [P, D])
        M_hi, M_lo = sb("M_hi", [P, DC, D], F32R), sb("M_lo", [P, DC, D], F32R)
        G_hi, G_lo = sb("G_hi", [P, DC, D], F32R), sb("G_lo", [P, DC, D], F32R)
        R_parts = sb("R_parts", [P, DC, 2, SM], F32R)
        small_w = sb("small_w", [P, DC, SM])
        xn_all = sb("xn_all", [P, NT, D])
        xn_cur = sb("xn_cur", [P, TPB, D])
        xnT_hi, xnT_lo = sb("xnT_hi", [P, DC, S], F32R), sb("xnT_lo", [P, DC, S], F32R)
        stats = sb("stats", [P, TPB, 6])
        mean_var = sb("mean_var", [P, TPB, 2])
        std = sb("std", [P, TPB])
        rstd = sb("rstd", [P, TPB])
        shift = sb("shift", [P, TPB])
        c_all = sb("c_all", [P, NT])
        slot_i = sb("slot_i", [P, NT], I32)
        slot_g = sb("slot_g", [P, NT], I32)
        first_tile = sb("first_tile", [P, E + 1], I32)
        last_tile = sb("last_tile", [P, E], I32)
        zero_row = sb("zero_row", [P, E], I32)
        tile_row = sb("tile_row", [P, TABLE], I32)
        qkvo_in, small_in, router_in, b2_in = sem("qkvo_in"), sem("small_in"), sem("router_in"), sem("b2_in")
        x_in = [sem(f"x_in{b}") for b in range(B)]
        x_ready = sem("x_ready")
        masks_ready, pool_step = sem("masks_ready"), sem("pool_step")
        dve_step = sem("dve_step")
        const_pe, const_act, const_dve = sem("const_pe"), sem("const_act"), sem("const_dve")
        zeros_ready, filled, tail_filled = sem("zeros_ready"), sem("filled"), sem("tail_filled")
        passed = sem("passed")
        var_ready, std_ready, ln_step = sem("var_ready"), sem("std_ready"), sem("ln_step")
        scales_ready, xn_ready, xn_kept = sem("scales_ready"), sem("xn_ready"), sem("xn_kept")
        lnT_done, lnT_hi, lnT_lo = sem("lnT_done"), sem("lnT_hi"), sem("lnT_lo")
        router_done, router_kept = sem("router_done"), sem("router_kept")
        logits_done, sort_step = sem("logits_done"), sem("sort_step")
        onehot_ready, ranks_done = sem("onehot_ready"), sem("ranks_done")
        carry_ready, counts_done = sem("carry_ready"), sem("counts_done")
        slots_ready, zero_rows_ready = sem("slots_ready"), sem("zero_rows_ready")
        tables_ready, slot_g_ready = sem("tables_ready"), sem("slot_g_ready")
        scattered = sem("scattered")
        w1_in, w2_in, b1_in, b1_ready = sem("w1_in"), sem("w2_in"), sem("b1_in"), sem("b1_ready")
        w1_high, w2_high = sem("w1_high"), sem("w2_high")
        w1_split, w2_split = sem("w1_split"), sem("w2_split")
        row_in, rowT_done, rowT_hi, rowT_ready = (sem("row_in"), sem("rowT_done"), sem("rowT_hi"),
                                                  sem("rowT_ready"))
        hid_done, hid_biased, gelu_done = sem("hid_done"), sem("hid_biased"), sem("gelu_done")
        hidT_done, hidT_hi0, hidT_hi1, hidT_ready = (sem("hidT_done"), sem("hidT_hi0"), sem("hidT_hi1"),
                                                     sem("hidT_ready"))
        y_done, y_biased, y_tanh, g_ready, g_stored = (sem("y_done"), sem("y_biased"),
                                                       sem("y_tanh"), sem("g_ready"),
                                                       sem("g_stored"))
        cur_in = sem("cur_in")
        prep_done, prep_hi, prep_ready = sem("prep_done"), sem("prep_hi"), sem("prep_ready")
        c_ready = sem("c_ready")
        scores_done, tanhs_done, acts_done = sem("scores_done"), sem("tanhs_done"), sem("acts_done")
        mixed, theta_done, exp_done = sem("mixed"), sem("theta_done"), sem("exp_done")
        pT_done, pT_hi0, pT_hi1, pT_ready = (sem("pT_done"), sem("pT_hi0"), sem("pT_hi1"),
                                             sem("pT_ready"))
        pv_done, rden_ready, half_s_ready = sem("pv_done"), sem("rden_ready"), sem("half_s_ready")
        slot_ready = sem("slot_ready")
        g_in = [sem("g_in0"), sem("g_in1")]
        xt_in = [sem("xt_in0"), sem("xt_in1")]
        out_sent = [sem("out_sent0"), sem("out_sent1")]
        scaled, out_ready = sem("scaled"), sem("out_ready")

        with ExitStack() as constants:
            def co(name, shape, dt=F32):
                return constants.enter_context(nc.sbuf_tensor(name, shape, dt))

            wq_raw, wv_raw = co("wq_raw", [P, DC, D]), co("wv_raw", [P, DC, D])
            wk_raw = co("wk_raw", [P, DC, D + 1])
            wo_raw, woT = co("wo_raw", [P, DC, D]), co("woT", [P, DC, D])
            bq_wide, bv_wide = co("bq_wide", [P, DC, P]), co("bv_wide", [P, DC, P])
        u_hi, u_lo = sb("u_hi", [P, DC, S], F32R), sb("u_lo", [P, DC, S], F32R)
        expert_id = sb("expert_id", [P, E, NT])
        expert_key = sb("expert_key", [P, E, TPB])
        tile_id = sb("tile_id", [P, TABLE])
        keep_scan = sb("keep_scan", [P, E, TPB + 1])
        logits = sb("logits", [P, 2, E, TPB])
        best = sb("best", [P, TPB])
        tagged = sb("tagged", [P, E, TPB])
        onehot = sb("onehot", [P, E, TPB + 1], F32R)
        running = sb("running", [P, E, TPB + 1], F32R)
        rank = sb("rank", [P, E, TPB])
        rank_all = sb("rank_all", [P, NT])
        tag_all = sb("tag_all", [P, NT])
        tiles_i = sb("tiles_i", [P, 2, E], I32)
        tiles_f = sb("tiles_f", [P, 3, E])
        gap = sb("gap", [P, E])
        last_used = sb("last_used", [P, 1])
        used_tile = sb("used_tile", [P, TABLE])
        after = sb("after", [P, E, TABLE])
        skipped = sb("skipped", [P, TABLE])
        first_slot = sb("first_slot", [P, NT])
        with ExitStack() as experts:
            def ex(name, shape, dt=F32):
                return experts.enter_context(nc.sbuf_tensor(name, shape, dt))

            w1_raw, w2_raw = ex("w1_raw", [P, DC, H]), ex("w2_raw", [P, HC, D])
            row = ex("row", [P, D])
            w1_hi = [ex(f"w1_hi{i}", [P, DC, H], F32R) for i in range(2)]
            w1_lo = [ex(f"w1_lo{i}", [P, DC, H], F32R) for i in range(2)]
            w2_hi = [ex(f"w2_hi{i}", [P, HC, D], F32R) for i in range(2)]
            w2_lo = [ex(f"w2_lo{i}", [P, HC, D], F32R) for i in range(2)]
            b1_all = [ex(f"b1_all{i}", [P, H]) for i in range(2)]
            rowT_h, rowT_l = ex("rowT_h", [P, DC, P], F32R), ex("rowT_l", [P, DC, P], F32R)
            hid = ex("hid", [P, H])
            router_T = hid[0:2 * SM, :]
            hidT_h, hidT_l = ex("hidT_h", [P, HC, P], F32R), ex("hidT_l", [P, HC, P], F32R)
            y_sb, y_t, g_sb = ex("y_sb", [P, D]), ex("y_t", [P, D]), ex("g_sb", [P, D])

        v_hi, v_lo = sb("v_hi", [P, TPB, VW], F32R), sb("v_lo", [P, TPB, VW], F32R)
        theta = sb("theta", [P, 2, S])
        tanh_s = sb("tanh_s", [P, S])
        relu_s = sb("relu_s", [P, S])
        neg_max = sb("neg_max", [P, 2, 2])
        pT_hi = [sb(f"pT_hi{i}", [P, TPB, P], F32R) for i in range(2)]
        pT_lo = [sb(f"pT_lo{i}", [P, TPB, P], F32R) for i in range(2)]
        c_cur = sb("c_cur", [P, 2, TPB])
        rden = sb("rden", [P, 2])
        half_s = sb("half_s", [P, 2, D])
        g_tile = sb("g_tile", [P, 2, D])
        x_tile = sb("x_tile", [P, 2, D])
        slot_cur = sb("slot_cur", [P, 2], I32)

        block = ctx.enter_context(nc.Block())

        chunked = lambda w: w.rearrange("(c p) n -> p c n", p=P)
        S_BANK, PT_BANK, O_BANK = 0, 4, 6
        ROUTER_BANKS = [4, 7]
        HID_BANK, HT_BANK, ROW_BANK, Y_BANK = 0, 2, 4, 5

        JT, JU, JV = 4, 4, TPB // 2
        JOBS = JT + JU + JV
        JV0, JV1 = range(JT + JU, JT + JU + JV // 2), range(JT + JU + JV // 2, JOBS)

        def prep_ps(q):
            if q < JT + JU:
                return ps[:, S_BANK + q % 4, :]
            return ps[:, PT_BANK + q - (JT + JU), :]

        KA = K_SIGMOID / 2
        KT, KR = K_TANH / KA, K_RELU / KA

        def halves(weights):
            chunks = weights.shape[1]
            return slice(0, chunks // 2), slice(chunks // 2, chunks)

        def wait_apart(engine, semaphore, value):
            engine.wait_ge(semaphore, value)
            engine.sem_inc(passed, 1)

        def zero_padding(engine, parity):
            engine.wait_ge(zeros_ready, 1)
            engine.wait_ge(zero_rows_ready, 1)
            for e in range(parity, E, 2):
                start = engine.value_load(zero_row[0:1, e:e + 1], min_val=0, max_val=E * REGION - P)
                engine.dma_start(sorted_x[bass.ds(start, P), :], zeros[:, :]).then_inc(filled, 16)

        @block.sync
        def _(sp):
            for first, src in ((BQ, bq), (BK, bk), (BV, bv)):
                sp.dma_start(bias_rows[first:first + DC, :], src.rearrange("(c p) -> c p", p=P)).then_inc(small_in, 16)
            for dst, src in ((wo_raw, Wo), (wk_raw, Wk), (wq_raw, Wq), (wv_raw, Wv)):
                sp.dma_start(dst[:, :, 0:D], chunked(src)).then_inc(qkvo_in, 16)
            for b in range(B):
                sp.dma_start(xn_all[:, b * TPB:(b + 1) * TPB, :],
                             x_rows[b * S:(b + 1) * S, :].rearrange("(i p) d -> p i d", p=P)
                             ).then_inc(x_in[b], 16)
            sp.dma_start(b2_all[:, :], b2.rearrange("e (a d) -> a (e d)", a=1).to_broadcast([P, E * D])
                         ).then_inc(b2_in, 16)
            for b in range(B):
                sp.wait_ge(x_in[b], 16)
                sp.sem_inc(x_ready, 1)
            sp.wait_ge(xn_kept, B)
            sp.wait_ge(lnT_hi, 4 * B)
            sp.dma_start(xn_cur[:, :, :], xn_all[:, 0:TPB, :]).then_inc(cur_in, 16)
            zero_padding(sp, 0)
            sp.wait_ge(tables_ready, 1)
            sp.wait_ge(filled, 16 * E)
            sp.wait_ge(scattered, 16 * NT)

            def load_row(t):
                start = sp.value_load(tile_row[0:1, bass.ds(t, 1)], min_val=0, max_val=E * REGION - P)
                sp.dma_start(row[:, :], sorted_x[bass.ds(start, P), :]).then_inc(row_in, 16)

            load_row(0)
            sp.dma_start(sorted_g[NT * P:, :].rearrange("(i p) d -> p i d", p=P),
                         zeros[:, :].rearrange("p (a d) -> p a d", a=1)
                         .to_broadcast([P, MAX_TILES - NT, D])).then_inc(tail_filled, 16)
            sp.wait_ge(rowT_done, 1)
            load_row(1)
            sp.wait_ge(tail_filled, 16)
            sp.sem_inc(g_stored, 16)
            def store_g(t):
                sp.wait_ge(g_ready, t + 1)
                sp.dma_start(sorted_g[bass.ds(t * P, P), :], g_sb[:, :]).then_inc(g_stored, 16)

            sp.wait_ge(rowT_done, 2)
            load_row(AHEAD)
            total = sp.value_load(first_tile[0:1, E:E + 1], min_val=E, max_val=MAX_TILES)
            with sp.Fori(1, total) as t:
                wait_apart(sp, rowT_done, t + AHEAD)
                load_row(t + AHEAD)
                store_g(t - 1)
            store_g(total - 1)
            for j in range(2):
                sp.dma_start(x_tile[:, j, :], x_rows[j * P:(j + 1) * P, :]).then_inc(xt_in[j], 16)

            def batch(b, last):
                if not last:
                    sp.wait_ge(prep_done, b * JOBS + JT)
                    sp.dma_start(xn_cur[:, :, :], xn_all[:, bass.ds(b * TPB + TPB, TPB), :]
                                 ).then_inc(cur_in, 16)
                for j in range(TPB):
                    sp.wait_ge(out_ready, b * TPB + j + 1)
                    sp.dma_start(out_rows[bass.ds(b * S + j * P, P), :], g_tile[:, j % 2, :]
                                 ).then_inc(out_sent[j % 2], 16)
                    if not (last and j + 2 >= TPB):
                        sp.dma_start(x_tile[:, j % 2, :], x_rows[bass.ds(b * S + (j + 2) * P, P), :]
                                     ).then_inc(xt_in[j % 2], 16)

            with sp.Fori(0, B - 1) as b:
                batch(b, False)
            batch(B - 1, True)
            for j in range(2):
                sp.wait_ge(out_sent[j], 16 * NT // 2)

        @block.gpsimd
        def _(pool):
            nc.gpsimd.memset(zeros[:, :], 0.0).then_inc(zeros_ready, 1)
            nc.gpsimd.memset(ident[:, :], 0.0).then_inc(pool_step, 1)
            nc.gpsimd.memset(before[:, :], 1.0).then_inc(pool_step, 1)
            pool.wait_ge(pool_step, 2)
            nc.gpsimd.affine_select(out=ident[:, :], in_=ident[:, :], compare_op=ALU.not_equal, fill=1.0,
                                    base=0, pattern=[[-1, P]], channel_multiplier=1).then_inc(masks_ready, 1)
            nc.gpsimd.affine_select(out=before[:, :], in_=before[:, :], compare_op=ALU.is_gt, fill=0.0,
                                    base=0, pattern=[[1, P]], channel_multiplier=-1).then_inc(masks_ready, 1)
            nc.gpsimd.iota(expert_key[:, :, :], pattern=[[1, E], [0, TPB]], base=E, channel_multiplier=0,
                           allow_small_or_imprecise_dtypes=True).then_inc(masks_ready, 1)
            nc.gpsimd.iota(expert_id[:, :, :], pattern=[[1, E], [0, NT]], base=0, channel_multiplier=0,
                           allow_small_or_imprecise_dtypes=True).then_inc(masks_ready, 1)
            nc.gpsimd.iota(tile_id[:, :], pattern=[[1, TABLE]], base=0, channel_multiplier=0,
                           allow_small_or_imprecise_dtypes=True).then_inc(masks_ready, 1)

            def load_w1(e):
                pool.dma_start(w1_raw[:, :, :], W1[bass.ds(e, 1)].rearrange(
                    "a (c p) n -> p (a c) n", p=P)).then_inc(w1_in, 16)

            def load_w2(e):
                pool.dma_start(w2_raw[:, :, :], W2[bass.ds(e, 1)].rearrange(
                    "a (c p) n -> p (a c) n", p=P)).then_inc(w2_in, 16)

            def load_b1(e, par):
                pool.dma_start(b1_all[par][:, :], b1[bass.ds(e, 1), :].to_broadcast([P, H])).then_inc(b1_in, 16)

            def low_weights(e, hi, lo, raw, high_done, split_done):
                for i, piece in enumerate(halves(raw)):
                    wait_apart(pool, high_done, e * 2 + i + 1)
                    last = nc.gpsimd.tensor_tensor(lo[:, piece, :], raw[:, piece, :], hi[:, piece, :].bitcast(F32),
                                                   ALU.subtract)
                last.then_inc(split_done, 1)
                wait_apart(pool, split_done, e + 1)

            def weights(e, par, free, more):
                if free:
                    tiles = pool.value_load(first_tile[0:1, bass.ds(e - 1, 1)], min_val=1, max_val=MAX_TILES)
                    wait_apart(pool, hid_biased, tiles * 2)
                load_b1(e, par)
                low_weights(e, w1_hi[par], w1_lo[par], w1_raw, w1_high, w1_split)
                pool.wait_ge(b1_in, e * 16 + 16)
                pool.sem_inc(b1_ready, 1)
                if more:
                    load_w1(e + 1)
                low_weights(e, w2_hi[par], w2_lo[par], w2_raw, w2_high, w2_split)
                if more:
                    load_w2(e + 1)

            pool.wait_ge(x_ready, 1)
            load_w1(0)
            load_w2(0)
            weights(0, 0, False, True)
            for b in range(B):
                pool.wait_ge(slots_ready, b + 1)
                pool.wait_ge(xn_kept, b + 1)
                for i in range(b * TPB, (b + 1) * TPB):
                    pool.indirect_dma_start(sorted_x, bass.IndirectOffsetOnAxis(ap=slot_i[:, i:i + 1], axis=0),
                                            xn_all[:, i, :], None).then_inc(scattered, 16)
            weights(1, 1, False, True)
            pool.wait_ge(tables_ready, 1)
            with pool.Fori(1, E // 2 - 1) as pair:
                for par in range(2):
                    weights(pair * 2 + par, par, True, True)
            for par in range(2):
                weights(E - 2 + par, par, True, par == 0)
            pool.sem_inc(w1_split, 1)
            pool.sem_inc(b1_ready, 1)

            total = pool.value_load(first_tile[0:1, E:E + 1], min_val=E, max_val=MAX_TILES)
            wait_apart(pool, g_stored, total * 16 + 16)
            pool.wait_ge(slot_g_ready, 1)

            def gather(n, par):
                nc.gpsimd.tensor_copy(slot_cur[:, par:par + 1], slot_g[:, bass.ds(n, 1)]).then_inc(slot_ready, 1)
                wait_apart(pool, slot_ready, n + 1)
                pool.indirect_dma_start(g_tile[:, par, :], None, sorted_g,
                                        bass.IndirectOffsetOnAxis(ap=slot_cur[:, par:par + 1], axis=0)
                                        ).then_inc(g_in[par], 16)

            for n in range(2):
                gather(n, n)
            pool.sem_inc(scaled, 2)

            def batch(b, last):
                for j in range(TPB):
                    n, par = b * TPB + j, j % 2
                    turn = b * (TPB // 2) + j // 2 + 1
                    pool.wait_ge(half_s_ready, n + 1)
                    pool.wait_ge(g_in[par], turn * 16)
                    nc.gpsimd.tensor_tensor(g_tile[:, par, :], half_s[:, par, :], g_tile[:, par, :],
                                            ALU.mult).then_inc(scaled, 1)
                    pool.wait_ge(scaled, n + 3)
                    pool.wait_ge(xt_in[par], turn * 16)
                    nc.gpsimd.tensor_tensor(g_tile[:, par, :], g_tile[:, par, :], x_tile[:, par, :],
                                            ALU.add).then_inc(out_ready, 1)
                    if not (last and j + 2 >= TPB):
                        wait_apart(pool, out_sent[par], turn * 16)
                        gather(n + 2, par)

            with pool.Fori(0, B - 1) as b:
                batch(b, False)
            batch(B - 1, True)

        @block.scalar
        def _(act):
            act.dma_start(bo_row[:, :], bo.rearrange("(a d) -> a d", a=1)).then_inc(router_in, 16)
            act.dma_start(br_all[:, :], br.rearrange("(a e) -> a e", a=1).to_broadcast([P, E])).then_inc(router_in, 16)
            act.dma_start(small_w[:, :, 0:E], chunked(Wr)).then_inc(router_in, 16)
            act.wait_ge(zeros_ready, 1)
            nc.scalar.activation(warm[:, 0:1], zeros[:, 0:1], ACT.Sqrt)
            def square_root(b):
                act.wait_ge(var_ready, b + 1)
                nc.scalar.activation(std[:, :], std[:, :], ACT.Sqrt).then_inc(std_ready, 1)

            def normalize(b):
                act.wait_ge(scales_ready, b + 1)
                for i in range(TPB):
                    last = nc.scalar.activation(xn_cur[:, i, :], xn_all[:, bass.ds(b * TPB + i, 1), :], ACT.Identity,
                                                scale=rstd[:, i:i + 1], bias=shift[:, i:i + 1])
                last.then_inc(xn_ready, 1)

            square_root(0)
            normalize(0)
            act.wait_ge(const_pe, 3)
            for m in range(DC):
                nc.scalar.activation(M_hi[:, m, :], ps[:, 4 + m, 0:D], ACT.Copy)
            nc.scalar.activation(G_hi[:, :, :], ps[:, 7, :].rearrange("p (m d) -> p m d", m=DC), ACT.Copy
                                 ).then_inc(const_act, 1)

            def ln_batch(b, more):
                for q in range(4):
                    act.wait_ge(lnT_done, b * 4 + q + 1)
                    nc.scalar.activation(xnT_hi[:, q % 2, (q // 2) * HALF:(q // 2 + 1) * HALF], ps[:, q, :],
                                         ACT.Copy).then_inc(lnT_hi, 1)
                if more:
                    square_root(b + 1)
                nc.scalar.activation(xn_all[:, bass.ds(b * TPB, TPB), :], xn_cur[:, :, :], ACT.Copy
                                     ).then_inc(xn_kept, 1)
                for h in range(2):
                    act.wait_ge(router_done, b * 2 + h + 1)
                    nc.scalar.activation(router_T[:, h * HALF:(h + 1) * HALF], ps[0:2 * SM, ROUTER_BANKS[h], :],
                                         ACT.Copy).then_inc(router_kept, 1)
                if more:
                    act.wait_ge(xn_kept, b + 1)
                    normalize(b + 1)

            def high_w1(e, par):
                act.wait_ge(w1_in, e * 16 + 16)
                for piece in halves(w1_raw):
                    nc.scalar.activation(w1_hi[par][:, piece, :], w1_raw[:, piece, :], ACT.Copy).then_inc(w1_high, 1)

            def high_w2(e, par, pieces=slice(0, 2)):
                act.wait_ge(w2_in, e * 16 + 16)
                for piece in halves(w2_raw)[pieces]:
                    nc.scalar.activation(w2_hi[par][:, piece, :], w2_raw[:, piece, :], ACT.Copy).then_inc(w2_high, 1)

            def high(n_batch, jobs):
                for q in jobs:
                    act.wait_ge(prep_done, n_batch * JOBS + q + 1)
                    if q < JT:
                        nc.scalar.activation(xnT_hi[:, q // 2, (q % 2) * HALF:(q % 2 + 1) * HALF], prep_ps(q),
                                             ACT.Copy).then_inc(prep_hi, 1)
                    elif q < JT + JU:
                        m, h = divmod(q - JT, 2)
                        nc.scalar.activation(u_hi[:, m, h * HALF:(h + 1) * HALF], prep_ps(q), ACT.Identity,
                                             bias=r_col[:, m:m + 1]).then_inc(prep_hi, 1)
                    else:
                        i = 2 * (q - JT - JU)
                        nc.scalar.activation(v_hi[:, i:i + 2, 0:D], prep_ps(q).rearrange("p (i d) -> p i d", d=D),
                                             ACT.Copy).then_inc(prep_hi, 1)

            ln_batch(0, True)
            high_w1(0, 0)
            high_w2(0, 0)
            with act.Fori(1, B - 1) as b:
                ln_batch(b, True)
            ln_batch(B - 1, False)

            def row_high(t):
                act.wait_ge(rowT_done, t + 1)
                nc.scalar.activation(rowT_h[:, :, :], ps[:, ROW_BANK, 0:D].rearrange("p (c n) -> p c n", c=DC),
                                     ACT.Copy).then_inc(rowT_hi, 1)

            def gelus(t, which=range(2)):
                for h in which:
                    part = hid[:, h * HALF:(h + 1) * HALF]
                    act.wait_ge(hid_biased, t * 2 + h + 1)
                    nc.scalar.activation(part, part, ACT.Gelu).then_inc(gelu_done, 1)

            nc.scalar.activation(warm[:, 1:2], zeros[:, 0:1], ACT.Gelu)
            high(0, range(0, JT))
            zero_padding(act, 1)
            high(0, range(JT, JT + JU))
            high_w1(1, 1)
            high_w2(1, 1)
            act.wait_ge(tables_ready, 1)
            row_high(0)
            gelus(0)
            row_high(1)

            def tile(t, weights=()):
                act.wait_ge(hidT_done, t * 2 + 2)
                nc.scalar.activation(hidT_h[:, HC // 2:, :], ps[:, HT_BANK + 1, :].rearrange(
                    "p (c n) -> p c n", n=P), ACT.Copy).then_inc(hidT_hi1, 1)
                if weights:
                    high_w1(*weights)
                gelus(t + 1, [0])
                if weights:
                    high_w2(*weights, slice(0, 1))
                gelus(t + 1, [1])
                row_high(t + AHEAD)
                if weights:
                    high_w2(*weights, slice(1, 2))
                act.wait_ge(y_biased, t + 1)
                nc.scalar.activation(y_t[:, :], y_sb[:, :], ACT.Tanh, scale=0.5).then_inc(y_tanh, 1)

            def first(e):
                return act.value_load(first_tile[0:1, bass.ds(e, 1)], min_val=0, max_val=MAX_TILES)

            t1 = first(1)
            with act.Fori(0, t1) as t:
                tile(t)
            with act.Fori(0, E // 2 - 1) as pair:
                for par in range(2):
                    e = pair * 2 + par + 1
                    t0 = t1 if par else first(e)
                    t1 = first(e + 1)
                    tile(t0, (e + 1, par))
                    with act.If(t0 + 1 < t1):
                        with act.Fori(t0 + 1, t1) as t:
                            tile(t)
            with act.Fori(t1, first(E)) as t:
                tile(t)
            nc.scalar.activation(warm[:, 2:3], zeros[:, 0:1], ACT.Exp)

            def tanhs(n, j, h):
                bank, cols = ps[:, S_BANK + 2 * (j % 2) + h, :], slice(h * HALF, (h + 1) * HALF)
                act.wait_ge(scores_done, n * 2 + h + 1)
                nc.scalar.activation(theta[:, j % 2, cols], bank, ACT.Tanh, bias=c_cur[:, 1, j:j + 1], scale=0.5)
                nc.scalar.activation(tanh_s[:, cols], bank, ACT.Tanh, bias=c_cur[:, 0, j:j + 1]
                                     ).then_inc(tanhs_done, 1)

            def relu(j, h):
                nc.scalar.activation(relu_s[:, h * HALF:(h + 1) * HALF], ps[:, S_BANK + 2 * (j % 2) + h, :], ACT.Relu,
                                     bias=c_cur[:, 0, j:j + 1], scale=KR).then_inc(acts_done, 1)

            def exps(n, j):
                act.wait_ge(theta_done, n + 1)
                for h in range(2):
                    part = theta[:, j % 2, h * HALF:(h + 1) * HALF]
                    nc.scalar.activation(part, part, ACT.Exp, bias=neg_max[:, j % 2, 1:2], scale=-1.0
                                         ).then_inc(exp_done, 1)

            assert KR == 1.0

            def acts(n, j):
                for h in range(2):
                    tanhs(n, j, h)
                    relu(j, h)

            def transposed_high(n, j):
                act.wait_ge(pT_done, n * 2 + 2)
                nc.scalar.activation(pT_hi[j % 2][:, TPB // 2:, :], ps[:, PT_BANK + 1, :].rearrange(
                    "p (c n) -> p c n", n=P), ACT.Copy).then_inc(pT_hi1, 1)

            def begin_batch(nb):
                act.wait_ge(c_ready, nb + 1)
                acts(nb * TPB, 0)
                high(nb, JV0)
                exps(nb * TPB, 0)

            def batch(b, last):
                for j in range(TPB):
                    n = b * TPB + j
                    if j + 1 < TPB:
                        acts(n + 1, j + 1)
                        if j == 0:
                            high(b, JV1)
                        transposed_high(n, j)
                        exps(n + 1, j + 1)
                    else:
                        if not last:
                            high(b + 1, range(0, JT))
                        transposed_high(n, j)
                        if not last:
                            high(b + 1, range(JT, JT + JU))
                            begin_batch(b + 1)

            begin_batch(0)
            with act.Fori(0, B - 1) as b:
                batch(b, False)
            batch(B - 1, True)

        @block.tensor
        def _(pe):
            mm = nc.tensor.matmul

            def product(dst, a_hi, a_lo, b_hi, b_lo, first, last):
                mm(dst, a_hi, b_hi, start=first, stop=False)
                mm(dst, a_hi, b_lo, start=False, stop=False)
                return mm(dst, a_lo, b_hi, start=False, stop=last)

            pe.wait_ge(masks_ready, 1)
            pe.wait_ge(small_in, 16 * 3)
            nr = 3 * DC
            nc.tensor.transpose(ps[:, 0, 0:nr], bias_rows[:, :], ident[0:nr, 0:nr]).then_inc(const_pe, 1)
            pe.wait_ge(qkvo_in, 16 * 4)
            for ec in range(DC):
                for fc in range(DC):
                    last = nc.tensor.transpose(ps[:, 1, ec * D + fc * P:ec * D + (fc + 1) * P],
                                               wo_raw[:, fc, ec * P:(ec + 1) * P], ident[:, :])
            last.then_inc(const_pe, 1)
            pe.wait_ge(const_dve, 1)
            for m in range(DC):
                for ec in range(DC):
                    mm(ps[:, 4 + m, 0:D + 1], wq_raw[:, ec, m * P:(m + 1) * P], wk_raw[:, ec, :],
                       start=ec == 0, stop=ec == DC - 1)
            for m in range(DC):
                for ec in range(DC):
                    mm(ps[:, 6, D + m:D + m + 1], wk_raw[:, ec, m * P:(m + 1) * P], bias_cols[:, BQ + ec:BQ + ec + 1],
                       start=ec == 0, stop=ec == DC - 1)
            for ec in range(DC):
                mm(ps[:, 6, D + DC:D + DC + 1], bq_wide[:, ec, :], bias_cols[:, BK + ec:BK + ec + 1],
                   start=ec == 0, stop=ec == DC - 1)
            for m in range(DC):
                for ec in range(DC):
                    mm(ps[:, 7, m * D:(m + 1) * D], wv_raw[:, ec, m * P:(m + 1) * P], woT[:, ec, :],
                       start=ec == 0, stop=ec == DC - 1)
            pe.wait_ge(router_in, 16 * 3)
            for ec in range(DC):
                mm(ps[:, 6, 0:D], bv_wide[:, ec, :], woT[:, ec, :], start=ec == 0, stop=False)
            mm(ps[:, 6, 0:D], ones[0:1, :], bo_row[:, :], start=False, stop=True).then_inc(const_pe, 1)

            def turn_batch(b):
                pe.wait_ge(xn_ready, b + 1)
                for q in range(4):
                    k, i0 = q % 2, (q // 2) * 4
                    for i in range(4):
                        last = nc.tensor.transpose(ps[:, q, i * P:(i + 1) * P],
                                                   xn_cur[:, i0 + i, k * P:(k + 1) * P], ident[:, :])
                    last.then_inc(lnT_done, 1)

            def route(b, more):
                for h in range(2):
                    pe.wait_ge(lnT_lo, b * 4 + h * 2 + 2)
                    cols, dst = slice(h * HALF, (h + 1) * HALF), ps[0:2 * SM, ROUTER_BANKS[h], :]
                    both = [R_parts[:, k, :, :].rearrange("p h s -> p (h s)") for k in range(DC)]
                    mm(dst, both[0], xnT_hi[:, 0, cols], start=True, stop=False)
                    for k in range(DC):
                        mm(dst[0:SM, :], R_parts[:, k, 0, :], xnT_lo[:, k, cols], start=False, stop=False)
                    mm(dst, both[1], xnT_hi[:, 1, cols], start=False, stop=True).then_inc(router_done, 1)
                for i in range(TPB):
                    if i % 4 == 0:
                        wait_apart(pe, router_kept, b * 2 + i // 4 + 1)
                    last = nc.tensor.transpose(ps[:, 6, i * 2 * SM:(i + 1) * 2 * SM], router_T[:, i * P:(i + 1) * P],
                                               ident[0:2 * SM, 0:2 * SM])
                last.then_inc(logits_done, 1)
                ranks = ps[:, 5, 0:E * TPB]
                pe.wait_ge(onehot_ready, b + 1)
                mm(ranks, before_r[:, :], onehot[:, :, 1:], start=True, stop=False)
                mm(ranks, ones_r[:, :], running[:, :, 0:TPB], start=False, stop=True).then_inc(ranks_done, 1)
                if more:
                    turn_batch(b + 1)
                else:
                    prepare(0, range(0, JT))

            def prepare(nb, jobs):
                for q in jobs:
                    bank = prep_ps(q)
                    if q < JT:
                        if q == 0:
                            pe.wait_ge(cur_in, nb * 16 + 16)
                        k, i0 = q // 2, (q % 2) * 4
                        for i in range(4):
                            last = nc.tensor.transpose(bank[:, i * P:(i + 1) * P],
                                                       xn_cur[:, i0 + i, k * P:(k + 1) * P], ident[:, :])
                    elif q < JT + JU:
                        if q == JT:
                            pe.wait_ge(prep_ready, nb * JOBS + JT)
                        m, h = divmod(q - JT, 2)
                        for k in range(DC):
                            rows, cols = slice(m * P, (m + 1) * P), slice(h * HALF, (h + 1) * HALF)
                            last = product(bank, M_hi[:, k, rows], M_lo[:, k, rows],
                                           xnT_hi[:, k, cols], xnT_lo[:, k, cols], k == 0, k == DC - 1)
                    else:
                        for i in range(2):
                            tile = 2 * (q - JT - JU) + i
                            cols = slice(tile * P, (tile + 1) * P)
                            for k in range(DC):
                                last = product(bank[:, i * D:(i + 1) * D], xnT_hi[:, k, cols], xnT_lo[:, k, cols],
                                               G_hi[:, k, :], G_lo[:, k, :], k == 0, k == DC - 1)
                    last.then_inc(prep_done, 1)

            turn_batch(0)
            pe.wait_ge(const_dve, 2)
            with pe.Fori(0, B - 1) as b:
                route(b, True)
            route(B - 1, False)
            pe.wait_ge(carry_ready, 1)
            mm(ps[:, 6, 0:E], ones_r[:, :], onehot[:, :, 0], start=True, stop=True).then_inc(counts_done, 1)

            def turn_row(t):
                pe.wait_ge(row_in, t * 16 + 16)
                for k in range(DC):
                    last = nc.tensor.transpose(ps[:, ROW_BANK, k * P:(k + 1) * P], row[:, k * P:(k + 1) * P],
                                               ident[:, :])
                last.then_inc(rowT_done, 1)

            def hidden(t, par):
                pe.wait_ge(rowT_ready, t + 1)
                for h in range(2):
                    for k in range(DC):
                        cols = slice(h * HALF, (h + 1) * HALF)
                        last = product(ps[:, HID_BANK + h, :], rowT_h[:, k, :], rowT_l[:, k, :],
                                       w1_hi[par][:, k, cols], w1_lo[par][:, k, cols], k == 0, k == DC - 1)
                    last.then_inc(hid_done, 1)

            def tile(t, e, par, ends):
                for h in range(2):
                    pe.wait_ge(gelu_done, t * 2 + h + 1)
                    for i in range(h * 4, h * 4 + 4):
                        last = nc.tensor.transpose(ps[:, HT_BANK + h, (i % 4) * P:(i % 4 + 1) * P],
                                                   hid[:, i * P:(i + 1) * P], ident[:, :])
                    last.then_inc(hidT_done, 1)
                if ends:
                    wait_apart(pe, w1_split, e + 2)
                hidden(t + 1, 1 - par if ends else par)
                turn_row(t + AHEAD)
                wait_apart(pe, w2_split, e + 1)
                for i in range(HC):
                    if i % 4 == 0:
                        pe.wait_ge(hidT_ready, t * 2 + i // 4 + 1)
                    last = product(ps[:, Y_BANK, 0:D], hidT_h[:, i, :], hidT_l[:, i, :],
                                   w2_hi[par][:, i, :], w2_lo[par][:, i, :], i == 0, i == HC - 1)
                last.then_inc(y_done, 1)

            prepare(0, range(JT, JT + JU))
            pe.wait_ge(tables_ready, 1)
            turn_row(0)
            pe.wait_ge(w1_split, 1)
            pe.wait_ge(prep_ready, JT + JU)
            hidden(0, 0)
            turn_row(1)
            with pe.Fori(0, E // 2) as pair:
                for par in range(2):
                    e = pair * 2 + par
                    t0 = t1 + 1 if par else pe.value_load(first_tile[0:1, bass.ds(e, 1)], min_val=0,
                                                          max_val=MAX_TILES - 1)
                    t1 = pe.value_load(last_tile[0:1, bass.ds(e, 1)], min_val=0, max_val=MAX_TILES - 1)
                    with pe.If(t0 < t1):
                        with pe.Fori(t0, t1) as t:
                            tile(t, e, par, False)
                    tile(t1, e, par, True)

            total = pe.value_load(first_tile[0:1, E:E + 1], min_val=E, max_val=MAX_TILES)
            wait_apart(pe, rowT_ready, total + AHEAD)

            def scores(n, j):
                for h in range(2):
                    for k in range(DC):
                        rows, cols = slice(j * P, (j + 1) * P), slice(h * HALF, (h + 1) * HALF)
                        last = product(ps[:, S_BANK + 2 * (j % 2) + h, :], u_hi[:, k, rows], u_lo[:, k, rows],
                                       xnT_hi[:, k, cols], xnT_lo[:, k, cols], k == 0, k == DC - 1)
                    last.then_inc(scores_done, 1)

            def transposes(n, j):
                for h in range(2):
                    pe.wait_ge(exp_done, n * 2 + h + 1)
                    for i in range(4):
                        last = nc.tensor.transpose(
                            ps[:, PT_BANK + h, i * P:(i + 1) * P],
                            theta[:, j % 2, h * HALF + i * P:h * HALF + (i + 1) * P], ident[:, :])
                    last.then_inc(pT_done, 1)

            def values(n, j):
                for i in range(TPB):
                    if i % 4 == 0:
                        pe.wait_ge(pT_ready, n * 2 + i // 4 + 1)
                    last = product(ps[:, O_BANK + j % 2, 0:VW], pT_hi[j % 2][:, i, :], pT_lo[j % 2][:, i, :],
                                   v_hi[:, i, :], v_lo[:, i, :], i == 0, i == TPB - 1)
                last.then_inc(pv_done, 1)

            def first_scores(nb):
                pe.wait_ge(prep_ready, nb * JOBS + JT + JU)
                scores(nb * TPB, 0)
                prepare(nb, JV0)

            def batch(b, last_batch):
                for j in range(TPB):
                    n = b * TPB + j
                    if j + 1 < TPB:
                        scores(n + 1, j + 1)
                        if j == 0:
                            pe.wait_ge(prep_ready, b * JOBS + JT + JU + len(JV0))
                            prepare(b, JV1)
                    elif not last_batch:
                        pe.wait_ge(acts_done, n * 2 + 2)
                        prepare(b + 1, range(0, JT))
                    if j + 1 == TPB:
                        values(n - 1, j - 1)
                    elif j > 0:
                        pe.wait_ge(pT_ready, n * 2)
                    transposes(n, j)
                    if j == 1:
                        pe.wait_ge(prep_ready, b * JOBS + JOBS)
                    if 0 < j < TPB - 1:
                        values(n - 1, j - 1)
                if not last_batch:
                    prepare(b + 1, range(JT, JT + JU))
                values(n, TPB - 1)
                if not last_batch:
                    first_scores(b + 1)

            scores(0, 0)
            wait_apart(pe, y_biased, total)
            prepare(0, JV0)
            with pe.Fori(0, B - 1) as b:
                batch(b, False)
            batch(B - 1, True)

        @block.vector
        def _(dve):
            v = nc.vector
            steps = [0]

            def step(ins):
                steps[0] += 1
                ins.then_inc(dve_step, 1)
                dve.wait_ge(dve_step, steps[0])

            v.memset(ones[:, :], 1.0)
            v.memset(keep_scan[:, :, :], 1.0)
            step(v.memset(small_w[:, :, E + 1:SM], 0.0))
            v.memset(onehot[:, :, 0:1].bitcast(F32), 0.0)
            step(v.memset(keep_scan[:, :, 0:1], 0.0))
            dve.wait_ge(const_pe, 1)
            step(v.tensor_copy(bias_cols[:, :], ps[:, 0, 0:3 * DC]))
            dve.wait_ge(qkvo_in, 16 * 4)
            for ec in range(DC):
                v.tensor_copy(wk_raw[:, ec, D:D + 1], bias_cols[:, BK + ec:BK + ec + 1])
                v.tensor_scalar(bq_wide[:, ec, :], ones[:, :], bias_cols[:, BQ + ec:BQ + ec + 1], None, ALU.mult)
                v.tensor_scalar(bv_wide[:, ec, :], ones[:, :], bias_cols[:, BV + ec:BV + ec + 1], None, ALU.mult)
            dve.wait_ge(const_pe, 2)
            v.tensor_copy(woT[:, :, :], ps[:, 1, :].rearrange("p (c f) -> p c f", c=DC)).then_inc(const_dve, 1)
            LN_STEPS, SORT_STEPS = 3, 9

            def statistics(b):
                dve.wait_ge(x_ready, b + 1)
                for i in range(TPB):
                    last = v.bn_stats(stats[:, i, :], xn_all[:, bass.ds(b * TPB + i, 1), :])
                last.then_inc(ln_step, 1)
                wait_apart(dve, ln_step, b * LN_STEPS + 1)
                for i in range(TPB):
                    last = v.bn_aggr(mean_var[:, i, :], stats[:, i, :])
                last.then_inc(ln_step, 1)
                dve.wait_ge(ln_step, b * LN_STEPS + 2)
                v.tensor_scalar(std[:, :], mean_var[:, :, 1], LN_EPS, None, ALU.add).then_inc(var_ready, 1)

            def scales(b):
                dve.wait_ge(std_ready, b + 1)
                v.reciprocal(rstd[:, :], std[:, :]).then_inc(ln_step, 1)
                wait_apart(dve, ln_step, b * LN_STEPS + 3)
                v.scalar_tensor_tensor(shift[:, :], mean_var[:, :, 0], -1.0, rstd[:, :], ALU.mult, ALU.mult
                                       ).then_inc(scales_ready, 1)

            dve.wait_ge(masks_ready, 5)
            v.tensor_copy(before_r[:, :], before[:, :])
            v.tensor_copy(ones_r[:, :], ones[:, :])
            statistics(0)
            scales(0)
            statistics(1)
            dve.wait_ge(const_pe, 3)
            dve.wait_ge(const_act, 1)
            dve.wait_ge(router_in, 16 * 3)
            for m in range(DC):
                v.tensor_copy(small_w[:, m, E:E + 1], ps[:, 4 + m, D:D + 1])
            v.tensor_copy(r_col[:, :], ps[:, 6, D:D + DC])
            v.tensor_copy(kappa[:, :], ps[:, 6, D + DC:D + DC + 1])
            step(v.tensor_scalar(attn_const[:, :], ps[:, 6, 0:D], 0.5, None, ALU.mult))
            step(v.tensor_copy(R_parts[:, :, 0, :], small_w[:, :, :]))
            v.tensor_tensor(R_parts[:, :, 1, :], small_w[:, :, :], R_parts[:, :, 0, :].bitcast(F32), ALU.subtract)
            for m in range(DC):
                v.tensor_tensor(M_lo[:, m, :], ps[:, 4 + m, 0:D], M_hi[:, m, :].bitcast(F32), ALU.subtract)
            v.tensor_tensor(G_lo[:, :, :], ps[:, 7, :].rearrange("p (m d) -> p m d", m=DC),
                            G_hi[:, :, :].bitcast(F32), ALU.subtract).then_inc(const_dve, 1)

            by_token = lambda a: a.rearrange("p e i -> p i e")
            over_experts = lambda a, n: a.rearrange("p (a i) -> p a i", a=1).to_broadcast([P, E, n])
            over_tiles = lambda a, n: a.rearrange("p (e a) -> p e a", a=1).to_broadcast([P, E, n])
            flat = lambda a: a[:, :, :].rearrange("p e i -> p (e i)")

            def route(b):
                count = [0]
                now = bass.ds(b * TPB, TPB)

                def then(ins):
                    count[0] += 1
                    ins.then_inc(sort_step, 1)
                    wait_apart(dve, sort_step, b * SORT_STEPS + count[0])

                dve.wait_ge(logits_done, b + 1)
                small = ps[:, 6, 0:TPB * 2 * SM].rearrange("p (i h s) -> p i h s", h=2, s=SM)
                v.tensor_scalar(c_all[:, now], small[:, :, 0, E], kappa[:, 0:1], None, ALU.add)
                then(v.tensor_tensor(by_token(logits[:, 0]), small[:, :, 0, 0:E],
                                     br_all[:, :].rearrange("p (a e) -> p a e", a=1).to_broadcast([P, TPB, E]),
                                     ALU.add))
                v.tensor_tensor(c_all[:, now], c_all[:, now], small[:, :, 1, E], ALU.add)
                then(v.tensor_tensor(by_token(logits[:, 1]), by_token(logits[:, 0]), small[:, :, 1, 0:E], ALU.add))
                then(v.tensor_reduce(best[:, :], by_token(logits[:, 1]), X, ALU.max))
                then(v.tensor_tensor(logits[:, 0], logits[:, 1], over_experts(best[:, :], TPB), ALU.is_ge))
                then(v.scalar_tensor_tensor(tagged[:, :, :], logits[:, 0], float(-E), expert_key[:, :, :],
                                            ALU.mult, ALU.add))
                then(v.tensor_reduce(tag_all[:, now], by_token(tagged[:, :, :]), X, ALU.min))
                then(v.tensor_tensor(onehot[:, :, 1:], tagged[:, :, :], over_experts(tag_all[:, now], TPB),
                                     ALU.is_equal))
                v.tensor_tensor_scan(flat(running), flat(keep_scan), flat(onehot).bitcast(F32), 0.0, ALU.mult, ALU.add
                                     ).then_inc(onehot_ready, 1)
                dve.wait_ge(ranks_done, b + 1)
                v.tensor_copy(onehot[:, :, 0], running[:, :, TPB].bitcast(F32))
                then(v.tensor_tensor(rank[:, :, :], ps[:, 5, 0:E * TPB].rearrange("p (e i) -> p e i", e=E),
                                     onehot[:, :, 1:].bitcast(F32), ALU.mult))
                then(v.tensor_reduce(rank_all[:, now], by_token(rank[:, :, :]), X, ALU.add))
                v.scalar_tensor_tensor(slot_i[:, now], tag_all[:, now], float(REGION), rank_all[:, now],
                                       ALU.mult, ALU.add).then_inc(slots_ready, 1)
                assert count[0] == SORT_STEPS

            def low_ln(b):
                for q in range(4):
                    cols = slice((q // 2) * HALF, (q // 2 + 1) * HALF)
                    dve.wait_ge(lnT_hi, b * 4 + q + 1)
                    v.tensor_tensor(xnT_lo[:, q % 2, cols], ps[:, q, :], xnT_hi[:, q % 2, cols].bitcast(F32),
                                    ALU.subtract).then_inc(lnT_lo, 1)

            def low(nb, jobs):
                for q in jobs:
                    dve.wait_ge(prep_hi, nb * JOBS + q + 1)
                    if q < JT:
                        cols = slice((q % 2) * HALF, (q % 2 + 1) * HALF)
                        v.tensor_tensor(xnT_lo[:, q // 2, cols], prep_ps(q), xnT_hi[:, q // 2, cols].bitcast(F32),
                                        ALU.subtract).then_inc(prep_ready, 1)
                    elif q < JT + JU:
                        m, h = divmod(q - JT, 2)
                        cols = slice(h * HALF, (h + 1) * HALF)
                        v.scalar_tensor_tensor(u_lo[:, m, cols], prep_ps(q), r_col[:, m:m + 1],
                                               u_hi[:, m, cols].bitcast(F32), ALU.add, ALU.subtract
                                               ).then_inc(prep_ready, 1)
                    else:
                        i = 2 * (q - JT - JU)
                        v.tensor_tensor(v_lo[:, i:i + 2, 0:D], prep_ps(q).rearrange("p (i d) -> p i d", d=D),
                                        v_hi[:, i:i + 2, 0:D].bitcast(F32), ALU.subtract).then_inc(prep_ready, 1)


            def ln_batch(b, left):
                low_ln(b)
                if left > 1:
                    scales(b + 1)
                if left > 2:
                    statistics(b + 2)
                route(b)

            with dve.Fori(0, B - 2) as b:
                ln_batch(b, 3)
            ln_batch(B - 2, 2)
            ln_batch(B - 1, 1)

            dve.sem_inc(carry_ready, 1)
            low(0, range(0, JT))
            dve.wait_ge(counts_done, 1)
            counts = ps[:, 6, 0:E]
            v.scalar_tensor_tensor(zero_row[:, :], expert_id[:, :, 0], float(REGION), counts, ALU.mult, ALU.add
                                   ).then_inc(zero_rows_ready, 1)
            step(v.tensor_scalar(tiles_i[:, 0, :], counts, float(P - 1), None, ALU.add))
            step(v.tensor_scalar(tiles_i[:, 1, :], tiles_i[:, 0, :], 7, None, ALU.arith_shift_right))
            step(v.tensor_scalar(tiles_f[:, 0, :], tiles_i[:, 1, :], 1.0, None, ALU.max))
            step(v.tensor_tensor_scan(tiles_f[:, 1, :], ones[:, 0:E], tiles_f[:, 0, :], 0.0, ALU.mult, ALU.add))
            v.memset(first_tile[:, 0:1], 0)
            v.memset(gap[:, 0:1], 0.0)
            v.tensor_copy(first_tile[:, 1:E + 1], tiles_f[:, 1, :])
            v.tensor_scalar(last_tile[:, :], tiles_f[:, 1, :], -1.0, None, ALU.add)
            v.tensor_scalar(last_used[:, :], tiles_f[:, 1, E - 1:E], -1.0, None, ALU.add)
            v.tensor_scalar(gap[:, 1:E], tiles_f[:, 0, 0:E - 1], float(-P), float(REGION), ALU.mult, ALU.add)
            step(v.tensor_tensor(tiles_f[:, 2, :], tiles_f[:, 1, :], tiles_f[:, 0, :], ALU.subtract))
            step(v.tensor_scalar(used_tile[:, :], tile_id[:, :], last_used[:, 0:1], None, ALU.min))
            step(v.tensor_tensor(after[:, :, :], over_experts(used_tile[:, :], TABLE),
                                 over_tiles(tiles_f[:, 2, :], TABLE), ALU.is_ge))
            step(v.tensor_tensor(after[:, :, :], after[:, :, :], over_tiles(gap[:, :], TABLE), ALU.mult))
            step(v.tensor_reduce(skipped[:, :], by_token(after[:, :, :]), X, ALU.add))
            v.scalar_tensor_tensor(tile_row[:, :], used_tile[:, :], float(P), skipped[:, :], ALU.mult, ALU.add
                                   ).then_inc(tables_ready, 1)
            chosen = after[:, :, 0:NT]
            step(v.tensor_tensor(chosen, over_experts(tag_all[:, :], NT), expert_id[:, :, :], ALU.is_equal))
            step(v.tensor_tensor(chosen, chosen, over_tiles(tiles_f[:, 2, :], NT), ALU.mult))
            step(v.tensor_reduce(first_slot[:, :], by_token(chosen), X, ALU.add))
            v.scalar_tensor_tensor(slot_g[:, :], first_slot[:, :], float(P), rank_all[:, :], ALU.mult, ALU.add
                                   ).then_inc(slot_g_ready, 1)

            def row_low(t):
                dve.wait_ge(rowT_hi, t + 1)
                v.tensor_tensor(rowT_l[:, :, :], ps[:, ROW_BANK, 0:D].rearrange("p (c n) -> p c n", c=DC),
                                rowT_h[:, :, :].bitcast(F32), ALU.subtract).then_inc(rowT_ready, 1)

            def add_b1(t, par):
                for h in range(2):
                    cols = slice(h * HALF, (h + 1) * HALF)
                    dve.wait_ge(hid_done, t * 2 + h + 1)
                    v.tensor_tensor(hid[:, cols], ps[:, HID_BANK + h, :], b1_all[par][:, cols], ALU.add
                                    ).then_inc(hid_biased, 1)

            def tile(t, e, next_par, ends=False):
                hid_bank = [ps[:, HT_BANK + h, :].rearrange("p (c n) -> p c n", n=P) for h in range(2)]
                dve.wait_ge(hidT_done, t * 2 + 1)
                v.tensor_copy(hidT_h[:, 0:4, :], hid_bank[0]).then_inc(hidT_hi0, 1)
                dve.wait_ge(hidT_hi0, t + 1)
                v.tensor_tensor(hidT_l[:, 0:4, :], hid_bank[0], hidT_h[:, 0:4, :].bitcast(F32), ALU.subtract
                                ).then_inc(hidT_ready, 1)
                dve.wait_ge(hidT_hi1, t + 1)
                v.tensor_tensor(hidT_l[:, 4:8, :], hid_bank[1], hidT_h[:, 4:8, :].bitcast(F32), ALU.subtract
                                ).then_inc(hidT_ready, 1)
                if ends:
                    wait_apart(dve, b1_ready, e + 2)
                add_b1(t + 1, next_par)
                row_low(t + AHEAD)
                dve.wait_ge(y_done, t + 1)
                v.tensor_tensor(y_sb[:, :], ps[:, Y_BANK, 0:D], b2_all[:, bass.ds(e * D, D)], ALU.add
                                ).then_inc(y_biased, 1)
                dve.wait_ge(y_tanh, t + 1)
                dve.wait_ge(g_stored, t * 16 + 16)
                v.scalar_tensor_tensor(g_sb[:, :], y_t[:, :], 1.0, y_sb[:, :], ALU.add, ALU.mult
                                       ).then_inc(g_ready, 1)

            low(0, range(JT, JT + JU))
            dve.wait_ge(slot_g_ready, 1)
            dve.wait_ge(b2_in, 16)
            dve.wait_ge(b1_ready, 1)
            row_low(0)
            add_b1(0, 0)
            row_low(1)
            with dve.Fori(0, E // 2) as pair:
                for par in range(2):
                    e = pair * 2 + par
                    t0 = t1 + 1 if par else dve.value_load(first_tile[0:1, bass.ds(e, 1)], min_val=0,
                                                           max_val=MAX_TILES - 1)
                    t1 = dve.value_load(last_tile[0:1, bass.ds(e, 1)], min_val=0, max_val=MAX_TILES - 1)
                    with dve.If(t0 < t1):
                        with dve.Fori(t0, t1) as t:
                            tile(t, e, par)
                    tile(t1, e, 1 - par, True)

            def batch_c(nb):
                v.tensor_copy(c_cur[:, 0, :], c_all[:, bass.ds(nb * TPB, TPB)])
                v.tensor_scalar(c_cur[:, 1, :], c_all[:, bass.ds(nb * TPB, TPB)], 0.5, None, ALU.mult
                                ).then_inc(c_ready, 1)

            def thetas(n, j):
                for h in range(2):
                    cols = slice(h * HALF, (h + 1) * HALF)
                    part = theta[:, j % 2, cols]
                    dve.wait_ge(tanhs_done, n * 2 + h + 1)
                    v.scalar_tensor_tensor(part, tanh_s[:, cols], KT, part, ALU.mult, ALU.add).then_inc(mixed, 1)
                    wait_apart(dve, mixed, n * 3 + 2 * h + 1)
                    wait_apart(dve, acts_done, n * 2 + h + 1)
                    least = neg_max[:, j % 2, h:h + 1]
                    ins = v.tensor_tensor_reduce(out=part, in0=part, in1=relu_s[:, cols], scale=-KA,
                                                 scalar=3.0e38 if h == 0 else neg_max[:, j % 2, 0:1],
                                                 op0=ALU.add, op1=ALU.min, accum_out=least)
                    ins.then_inc(mixed if h == 0 else theta_done, 1)
                    if h == 0:
                        wait_apart(dve, mixed, n * 3 + 2)

            def finish(n, j):
                dve.wait_ge(pv_done, n + 1)
                v.reciprocal(rden[:, j % 2:j % 2 + 1], ps[:, O_BANK + j % 2, D:D + 1]).then_inc(rden_ready, 1)
                dve.wait_ge(rden_ready, n + 1)
                dve.wait_ge(scaled, n + 1)
                v.scalar_tensor_tensor(half_s[:, j % 2, :], ps[:, O_BANK + j % 2, 0:D], rden[:, j % 2:j % 2 + 1], attn_const[:, :],
                                       ALU.mult, ALU.add).then_inc(half_s_ready, 1)

            def transposed_parts(n, j):
                dve.wait_ge(pT_done, n * 2 + 1)
                bank = [ps[:, PT_BANK + h, :].rearrange("p (c n) -> p c n", n=P) for h in range(2)]
                hi, lo = pT_hi[j % 2], pT_lo[j % 2]
                v.tensor_copy(hi[:, 0:4, :], bank[0]).then_inc(pT_hi0, 1)
                dve.wait_ge(pT_hi0, n + 1)
                v.tensor_tensor(lo[:, 0:4, :], bank[0], hi[:, 0:4, :].bitcast(F32), ALU.subtract).then_inc(pT_ready, 1)
                dve.wait_ge(pT_hi1, n + 1)
                v.tensor_tensor(lo[:, 4:8, :], bank[1], hi[:, 4:8, :].bitcast(F32), ALU.subtract).then_inc(pT_ready, 1)

            def batch(b, last):
                for j in range(TPB):
                    n = b * TPB + j
                    if j + 1 < TPB:
                        thetas(n + 1, j + 1)
                        if j == 0:
                            low(b, JV1)
                    elif not last:
                        low(b + 1, range(0, JT))
                    transposed_parts(n, j)
                    if j:
                        finish(n - 1, j - 1)
                if not last:
                    low(b + 1, range(JT, JT + JU))
                    batch_c(b + 1)
                finish(n, TPB - 1)
                if not last:
                    thetas(n + 1, 0)
                    low(b + 1, JV0)

            v.memset(v_hi[:, :, D:D + 1].bitcast(F32), 2.0)
            v.memset(v_hi[:, :, D + 1:VW].bitcast(F32), 0.0)
            v.memset(v_lo[:, :, D:VW].bitcast(F32), 0.0)
            batch_c(0)
            thetas(0, 0)
            low(0, JV0)
            with dve.Fori(0, B - 1) as b:
                batch(b, False)
            batch(B - 1, True)


_INS = ['L0_attn_x', 'L0_attn_Wq', 'L0_attn_bq', 'L0_attn_Wk', 'L0_attn_bk', 'L0_attn_Wv', 'L0_attn_bv', 'L0_attn_Wo',
        'L0_attn_bo', 'L0_ffn_Wr', 'L0_ffn_br', 'L0_ffn_W1', 'L0_ffn_b1', 'L0_ffn_W2', 'L0_ffn_b2']


def kernel(**inputs):
    import numpy as _np
    import concourse.bacc as _bacc
    from concourse import mybir as _mybir
    from concourse.bass_utils import run_bass_kernel_spmd as _run

    nc = _bacc.Bacc("TRN2", target_bir_lowering=False, num_devices=1)
    arrays, args = {}, []
    for name in _INS:
        a = _np.ascontiguousarray(inputs[name])
        arrays[f"in_{name}_dram"] = a
        args.append(nc.dram_tensor(f"in_{name}_dram", a.shape, _mybir.dt.from_np(a.dtype), kind="ExternalInput").ap())
    shape = tuple(inputs['L0_attn_x'].shape)
    args.append(nc.dram_tensor("out_0_dram", shape, F32, kind="ExternalOutput").ap())
    block_attention_moe(nc, *args)
    r = _run(nc, [arrays], core_ids=[0])
    return r.results[0]["out_0_dram"]
```
